# Optimizing a Trainium2 kernel written in Bass

```python
import numpy as np
import jax
import jax.numpy as jnp

def _softmax(x, axis=-1):
    return jax.nn.softmax(x, axis=axis)

def _gelu(x):
    return jax.nn.gelu(x, approximate=True)

def _silu(x):
    return jax.nn.silu(x)

def _sigmoid(x):
    return jax.nn.sigmoid(x)

def _layernorm(x, axis=-1, eps=1e-05):
    m = jnp.mean(x, axis=axis, keepdims=True)
    v = jnp.var(x, axis=axis, keepdims=True)
    return (x - m) / jnp.sqrt(v + eps)

def _scatter_add(tgt, idx, src, axis=0):
    return tgt.at[idx].add(src)

def _segment_sum(src, seg, n):
    return jax.ops.segment_sum(src, seg, n)
kernel_name = 'mk_gnn_resnorm_d4_gnn_r8_254655'

def setup_inputs(seed: int=0):
    np.random.seed(seed)
    _w = jnp.asarray

    def _rec_inputs():
        import jax
        import jax.numpy as jnp
        _gk = jax.random.key(seed)
        x = -0.0005121 + 1.001 * jax.random.normal(jax.random.fold_in(_gk, 1), (6250, 64), jnp.float32)
        _s = jax.random.randint(jax.random.fold_in(_gk, 2), (100000,), 0, 6250, jnp.int32)
        _d = jax.random.randint(jax.random.fold_in(_gk, 3), (100000,), 0, 6250, jnp.int32)
        _loop = jnp.arange(6250, dtype=jnp.int32)
        src = jnp.concatenate([_s, _d, _loop])
        dst = jnp.concatenate([_d, _s, _loop])
        _o = jnp.argsort(dst, stable=True)
        src = src[_o]
        dst = dst[_o]
        edge_weight = jax.random.uniform(jax.random.fold_in(_gk, 13), (206250,), jnp.float32, 0.0, 1)
        return (x, src, dst, edge_weight)
    x, src, dst, edge_weight = _rec_inputs()

    def _L0_gnn_setup():
        import jax, jax.numpy as jnp
        import numpy as np
        N = 6250
        E = 100000
        D_IN = 64
        D_HID = 64
        D_OUT = 64

        def graph_conv(x, src, dst, W_rel, W_root, b):
            agg = jax.ops.segment_sum(x[src], dst, num_segments=N)
            return agg @ W_rel + b + x @ W_root
        key = jax.random.key(seed)
        ks = jax.random.split(key, 8)
        x = jax.random.normal(ks[0], (N, D_IN), dtype=jnp.float32)
        edge_index = jax.random.randint(ks[1], (2, E), 0, N, dtype=jnp.int64)
        s = 1.0 / np.sqrt(D_IN)
        W1_rel = jax.random.uniform(ks[2], (D_IN, D_HID), minval=-s, maxval=s, dtype=jnp.float32)
        W1_root = jax.random.uniform(ks[3], (D_IN, D_HID), minval=-s, maxval=s, dtype=jnp.float32)
        b1 = jax.random.uniform(ks[4], (D_HID,), minval=-s, maxval=s, dtype=jnp.float32)
        s2 = 1.0 / np.sqrt(D_HID)
        W2_rel = jax.random.uniform(ks[5], (D_HID, D_OUT), minval=-s2, maxval=s2, dtype=jnp.float32)
        W2_root = jax.random.uniform(ks[6], (D_HID, D_OUT), minval=-s2, maxval=s2, dtype=jnp.float32)
        b2 = jax.random.uniform(ks[7], (D_OUT,), minval=-s2, maxval=s2, dtype=jnp.float32)
        return {'x': x, 'edge_index': edge_index, 'W1_rel': W1_rel, 'W1_root': W1_root, 'b1': b1, 'W2_rel': W2_rel, 'W2_root': W2_root, 'b2': b2}
    _L0_gnn_all = _L0_gnn_setup()
    _L0_gnn_in = {k: v for k, v in _L0_gnn_all.items() if k in ('W1_rel', 'W1_root', 'b1', 'W2_rel', 'W2_root', 'b2')}
    del _L0_gnn_all

    def _L1_gnn_setup():
        import jax, jax.numpy as jnp
        import numpy as np
        N = 12500
        E = 125000
        D = 64
        L = 2

        def _safediv(a, b):
            return a / jnp.where(b == 0, jnp.ones_like(b), b)
        key = jax.random.key(seed)
        ks = jax.random.split(key, 4 + 2 * L)
        inp = {'x': jax.random.normal(ks[0], (N, D), jnp.float32), 'ppr_weight': jax.random.uniform(ks[1], (E,), jnp.float32), 'src': jax.random.randint(ks[2], (E,), 0, N), 'dst': jnp.sort(jax.random.randint(ks[3], (E,), 0, N))}
        for i in range(L):
            inp[f'Qw{i}'] = jax.random.normal(ks[4 + 2 * i], (D, D), jnp.float32) / jnp.sqrt(D).astype(jnp.float32)
            inp[f'Qb{i}'] = jnp.zeros((D,), jnp.float32)
            inp[f'Ww{i}'] = jax.random.normal(ks[5 + 2 * i], (D, 2 * D), jnp.float32) / jnp.sqrt(2.0 * D).astype(jnp.float32)
            inp[f'Wb{i}'] = jnp.zeros((D,), jnp.float32)
        return inp
    _L1_gnn_all = _L1_gnn_setup()
    _L1_gnn_in = {k: v for k, v in _L1_gnn_all.items() if k in ('Qw0', 'Qb0', 'Ww0', 'Wb0', 'Qw1', 'Qb1', 'Ww1', 'Wb1')}
    del _L1_gnn_all

    def _L2_gnn_setup():
        import jax, jax.numpy as jnp
        import numpy as np
        N_USERS = 52643
        N_ITEMS = 91599
        N = N_USERS + N_ITEMS
        M_PAIRS = 125000
        D = 64
        key = jax.random.key(seed)
        k1, k2, k3, k4, k5 = jax.random.split(key, 5)
        u = jax.random.randint(k1, (M_PAIRS,), 0, N_USERS, dtype=jnp.int32)
        it = jax.random.randint(k2, (M_PAIRS,), N_USERS, N, dtype=jnp.int32)
        row = jnp.concatenate([u, it])
        col = jnp.concatenate([it, u])
        embed = jax.random.normal(k3, (N, D), dtype=jnp.float32)
        W1 = jax.random.normal(k4, (D, D), dtype=jnp.float32) * 0.01
        W2 = jax.random.normal(k5, (D, D), dtype=jnp.float32) * 0.01
        b1 = jnp.zeros((D,), jnp.float32)
        b2 = jnp.zeros((D,), jnp.float32)
        return {'embed': embed, 'row': row, 'col': col, 'W1': W1, 'b1': b1, 'W2': W2, 'b2': b2}
    _L2_gnn_all = _L2_gnn_setup()
    _L2_gnn_in = {k: v for k, v in _L2_gnn_all.items() if k in ('W1', 'b1', 'W2', 'b2')}
    del _L2_gnn_all

    def _L3_gnn_setup():
        import jax, jax.numpy as jnp
        import numpy as np
        N_NODES = 6250
        key = jax.random.key(seed)
        k_x, k_e, k_w1, k_b1, k_w2, k_b2 = jax.random.split(key, 6)
        C_in, C_out = (64, 64)
        E = 200000
        x = jax.random.normal(k_x, (N_NODES, C_in), dtype=jnp.float32)
        edge_index = jax.random.randint(k_e, (2, E), 0, N_NODES, dtype=jnp.int64)
        s1 = 1.0 / np.sqrt(2 * C_in)
        s2 = 1.0 / np.sqrt(C_out)
        W1 = jax.random.uniform(k_w1, (2 * C_in, C_out), jnp.float32, -s1, s1)
        b1 = jax.random.uniform(k_b1, (C_out,), jnp.float32, -s1, s1)
        W2 = jax.random.uniform(k_w2, (C_out, C_out), jnp.float32, -s2, s2)
        b2 = jax.random.uniform(k_b2, (C_out,), jnp.float32, -s2, s2)
        return {'x': x, 'edge_index': edge_index, 'W1': W1, 'b1': b1, 'W2': W2, 'b2': b2}
    _L3_gnn_all = _L3_gnn_setup()
    _L3_gnn_in = {k: v for k, v in _L3_gnn_all.items() if k in ('W1', 'b1', 'W2', 'b2')}
    del _L3_gnn_all
    return {'x': x, 'src': src, 'dst': dst, 'edge_weight': edge_weight, 'L0_gnn_W1_rel': _L0_gnn_in['W1_rel'], 'L0_gnn_W1_root': _L0_gnn_in['W1_root'], 'L0_gnn_b1': _L0_gnn_in['b1'], 'L0_gnn_W2_rel': _L0_gnn_in['W2_rel'], 'L0_gnn_W2_root': _L0_gnn_in['W2_root'], 'L0_gnn_b2': _L0_gnn_in['b2'], 'L1_gnn_Qw0': _L1_gnn_in['Qw0'], 'L1_gnn_Qb0': _L1_gnn_in['Qb0'], 'L1_gnn_Ww0': _L1_gnn_in['Ww0'], 'L1_gnn_Wb0': _L1_gnn_in['Wb0'], 'L1_gnn_Qw1': _L1_gnn_in['Qw1'], 'L1_gnn_Qb1': _L1_gnn_in['Qb1'], 'L1_gnn_Ww1': _L1_gnn_in['Ww1'], 'L1_gnn_Wb1': _L1_gnn_in['Wb1'], 'L2_gnn_W1': _L2_gnn_in['W1'], 'L2_gnn_b1': _L2_gnn_in['b1'], 'L2_gnn_W2': _L2_gnn_in['W2'], 'L2_gnn_b2': _L2_gnn_in['b2'], 'L3_gnn_W1': _L3_gnn_in['W1'], 'L3_gnn_b1': _L3_gnn_in['b1'], 'L3_gnn_W2': _L3_gnn_in['W2'], 'L3_gnn_b2': _L3_gnn_in['b2']}

def reference(x, src, dst, edge_weight, L0_gnn_W1_rel, L0_gnn_W1_root, L0_gnn_b1, L0_gnn_W2_rel, L0_gnn_W2_root, L0_gnn_b2, L1_gnn_Qw0, L1_gnn_Qb0, L1_gnn_Ww0, L1_gnn_Wb0, L1_gnn_Qw1, L1_gnn_Qb1, L1_gnn_Ww1, L1_gnn_Wb1, L2_gnn_W1, L2_gnn_b1, L2_gnn_W2, L2_gnn_b2, L3_gnn_W1, L3_gnn_b1, L3_gnn_W2, L3_gnn_b2):
    import jax
    import jax.numpy as jnp

    def _L0_gnn_ref(x, edge_index, W1_rel, W1_root, b1, W2_rel, W2_root, b2):
        import jax, jax.numpy as jnp
        import numpy as np
        N = 6250
        E = 100000
        D_IN = 64
        D_HID = 64
        D_OUT = 64

        def graph_conv(x, src, dst, W_rel, W_root, b):
            agg = jax.ops.segment_sum(x[src], dst, num_segments=N)
            return agg @ W_rel + b + x @ W_root
        src, dst = (edge_index[0], edge_index[1])
        h = jax.nn.relu(graph_conv(x, src, dst, W1_rel, W1_root, b1))
        out = jax.nn.relu(graph_conv(h, src, dst, W2_rel, W2_root, b2))
        return out

    def _L1_gnn_ref(x, ppr_weight, src, dst, Qw0, Qb0, Ww0, Wb0, Qw1, Qb1, Ww1, Wb1):
        import jax, jax.numpy as jnp
        import numpy as np
        N = 12500
        E = 125000
        D = 64
        L = 2

        def _safediv(a, b):
            return a / jnp.where(b == 0, jnp.ones_like(b), b)
        params = [(Qw0, Qb0, Ww0, Wb0), (Qw1, Qb1, Ww1, Wb1)]
        n = x.shape[0]
        h = x
        for Qw, Qb, Ww, Wb in params:
            h_q = jax.nn.leaky_relu(h @ Qw.T + Qb)
            msg = h_q[src] * ppr_weight[:, None]
            h_agg = jax.ops.segment_sum(msg, dst, num_segments=n)
            wsum = jax.ops.segment_sum(ppr_weight, dst, num_segments=n)
            h_agg = _safediv(h_agg, wsum[:, None])
            h_new = jax.nn.leaky_relu(jnp.concatenate([h, h_agg], axis=1) @ Ww.T + Wb)
            nrm = jnp.linalg.norm(h_new, axis=1, keepdims=True)
            h = _safediv(h_new, nrm)
        return h

    def _L2_gnn_ref(embed, row, col, W1, b1, W2, b2):
        import jax, jax.numpy as jnp
        import numpy as np
        N_USERS = 52643
        N_ITEMS = 91599
        N = N_USERS + N_ITEMS
        M_PAIRS = 125000
        D = 64
        n = embed.shape[0]
        deg = jax.ops.segment_sum(jnp.ones(row.shape, embed.dtype), row, num_segments=n)
        dinv = jnp.where(deg > 0, jax.lax.rsqrt(jnp.maximum(deg, 1.0)), 0.0)
        vals = dinv[row] * dinv[col]

        def spmm(x):
            return jax.ops.segment_sum(vals[:, None] * x[col], row, num_segments=n)
        h1 = embed + spmm(embed)
        h2 = spmm(embed * embed)
        return h1 @ W1.T + b1 + (h2 @ W2.T + b2)

    def _L3_gnn_ref(x, edge_index, W1, b1, W2, b2):
        import jax, jax.numpy as jnp
        import numpy as np
        N_NODES = 6250
        i = edge_index[0]
        j = edge_index[1]
        x_i = x[i]
        x_j = x[j]
        edge_feat = jnp.concatenate([x_i, x_j - x_i], axis=-1)
        h = jax.nn.relu(edge_feat @ W1 + b1)
        messages = jax.nn.relu(h @ W2 + b2)
        out = jax.ops.segment_sum(messages, j, num_segments=N_NODES)
        ones = jnp.ones((j.shape[0],), dtype=jnp.float32)
        deg = jax.ops.segment_sum(ones, j, num_segments=N_NODES)
        deg = jnp.maximum(deg, 1.0)[:, None]
        return out / deg
    edge_index = jnp.stack([src, dst])
    x = _layernorm(x + _L0_gnn_ref(x, edge_index, L0_gnn_W1_rel, L0_gnn_W1_root, L0_gnn_b1, L0_gnn_W2_rel, L0_gnn_W2_root, L0_gnn_b2), axis=-1)
    x = _layernorm(x + _L1_gnn_ref(x, edge_weight, src, dst, L1_gnn_Qw0, L1_gnn_Qb0, L1_gnn_Ww0, L1_gnn_Wb0, L1_gnn_Qw1, L1_gnn_Qb1, L1_gnn_Ww1, L1_gnn_Wb1), axis=-1)
    x = _layernorm(x + _L2_gnn_ref(x, src, dst, L2_gnn_W1, L2_gnn_b1, L2_gnn_W2, L2_gnn_b2), axis=-1)
    x = _layernorm(x + _L3_gnn_ref(x, edge_index, L3_gnn_W1, L3_gnn_b1, L3_gnn_W2, L3_gnn_b2), axis=-1)
    return x

_drawn_inputs = setup_inputs


def setup_inputs(seed=0):
    import zlib

    import numpy as np

    out = dict(_drawn_inputs(seed))
    spreads = {'L1_gnn_Qb0': (0.0, 2.0),
     'L1_gnn_Wb0': (0.0, 0.8),
     'L1_gnn_Qb1': (0.0, 0.1),
     'L1_gnn_Wb1': (0.0, 0.1),
     'L2_gnn_b1': (0.0, 0.1),
     'L2_gnn_b2': (0.0, 0.1)}
    factors = {'edge_weight': 64.0, 'L0_gnn_b2': 8.0, 'L3_gnn_b1': 4.817, 'L1_gnn_Qw0': 3.023}
    for name, (base, spread) in spreads.items():
        noise = np.random.default_rng([zlib.crc32(name.encode()), seed]).standard_normal(out[name].shape)
        drawn = base * np.exp(spread * noise) if base else spread * noise
        out[name] = jnp.asarray(drawn.astype(out[name].dtype))
    for name, factor in factors.items():
        out[name] = (out[name] * factor).astype(out[name].dtype)
    return out
```

```python
import numpy as np
import concourse.bass as bass
from concourse import mybir
from concourse.alu_op_type import AluOpType as ALU

F32, I32, BF16 = mybir.dt.float32, mybir.dt.int32, mybir.dt.bfloat16
ACT = mybir.ActivationFunctionType
AX = mybir.AxisListType
PE_ENGINE, ACT_ENGINE, DVE_ENGINE = (
    mybir.EngineType.PE, mybir.EngineType.Activation, mybir.EngineType.DVE)

P = 128
N_NODES, N_EDGES, D = 6250, 206250, 64
BLOCKS = -(-N_NODES // P)
COLS = -(-N_EDGES // P)
G, SLOTS = 8, 4
ROUND = G * SLOTS
TILES = -(-(COLS + BLOCKS) // ROUND) * ROUND
ROUNDS = TILES // ROUND
GROUPS = TILES // G
G0 = 13
ROUNDS0 = COLS // (G0 * SLOTS)
BK = ROUNDS
TCH = TILES // P
BANK = 512
PER_BANK, ACC = 7, 72
NBANK = BLOCKS // PER_BANK
LAST_PLACE = (NBANK - 1) * BANK + (PER_BANK - 1) * ACC
ROW = D + 1
PAD_NODE, PAD_LOW = 8191, 200.0
CH = 4
CHUNKS = -(-BLOCKS // CH)
LAYERS = 6
EPS, SLOPE = 1e-5, 0.01
assert COLS == G0 * SLOTS * ROUNDS0 and NBANK * PER_BANK == BLOCKS and TCH * P == TILES
assert BK >= BLOCKS and P * BLOCKS <= PAD_NODE < P * 64

MATS = ["c1_rel", "c1_root", "c2_rel", "c2_root", "q0", "wa0", "wb0", "q1", "wa1", "wb1",
        "bi1", "bi2", "e1a", "e1b", "e2"]
ROWS = ["c1", "c2", "w0", "w1", "bi1", "bi2", "e1"]


class Steps:

    def __init__(self, engine, sem):
        self.engine, self.sem, self.n = engine, sem, 0

    def __call__(self, instruction):
        instruction.then_inc(self.sem, 1)
        self.n = self.n + 1
        self.engine.wait_ge(self.sem, self.n)

    def loop(self, count, each, body):
        first = self.n
        with self.engine.Fori(0, count) as i:
            self.n = first + i * each
            body(i)
        self.n = first + count * each


ROWS_IN = TILES + 2


def build(nc, x_in, src_in, dst_in, w_in, mats_in, rows_in, qb_in, e2b_in, out):
    from contextlib import ExitStack
    ctx = ExitStack()
    with ctx:
        def sb(name, shape, dt=F32):
            return ctx.enter_context(nc.sbuf_tensor(name, shape, dt))

        def sem(name):
            return ctx.enter_context(nc.semaphore(name))

        table = nc.dram_tensor("table", [P * BLOCKS, D], F32, kind="Internal").ap()
        slots_d = nc.dram_tensor("slots_d", [P * TILES, 3], F32, kind="Internal").ap()
        rows_d = nc.dram_tensor("rows_d", [P * TILES, ROW], F32, kind="Internal").ap()
        low_d = nc.dram_tensor("low_d", [TILES, P], F32, kind="Internal").ap()
        place_d = nc.dram_tensor("place_d", [3, TCH, P], I32, kind="Internal").ap()

        row_iota = sb("row_iota", [P, P])
        part_iota = sb("part_iota", [P, 1])
        block_iota = sb("block_iota", [P, BK])
        tile_iota = sb("tile_iota", [P, TCH])
        ident = sb("ident", [P, P])
        before = sb("before", [P, P])
        ones = sb("ones", [P, P])
        zeros = sb("zeros", [P, BANK])
        mats = sb("mats", [D, len(MATS), D])
        rows = sb("rows", [P, len(ROWS), D])
        qb = sb("qb", [D, 2])
        bi_stack = sb("bi_stack", [P, D])
        edge_w = sb("edge_w", [D, 2, D])
        e2 = sb("e2", [ROW, D])

        def rectangle(rows):
            return rows.rearrange("r e -> (r e)")[0:P * COLS].rearrange("(p j) -> p j", p=P)

        wide = sb("wide", [P, 2 * SLOTS * G * P])
        src_i = wide[:, 0:COLS].bitcast(I32)
        dst_i = wide[:, COLS:2 * COLS].bitcast(I32)
        w_raw = wide[:, 2 * COLS:3 * COLS]
        hotT = wide[:, 0:SLOTS * G * P].rearrange("p (s e) -> p s e", s=SLOTS)
        lowT = wide[:, SLOTS * G * P:].rearrange("p (s e) -> p s e", s=SLOTS)
        half = wide[:, :].bitcast(BF16)
        src_hot = half[:, 0:SLOTS * G * P].rearrange("p (s g e) -> p s g e", s=SLOTS, g=G)
        src_blk = half[:, SLOTS * G * P:SLOTS * G * (P + BLOCKS)]\
            .rearrange("p (s g b) -> p s g b", s=SLOTS, g=G)
        low_turn = wide[:, 0:4 * P].rearrange("p (a e) -> p a e", e=P)
        pairs = wide[:, 0:BLOCKS * 2 * D].rearrange("p (b f) -> p b f", b=BLOCKS)

        sorting = sb("sorting", [P, 4, TILES])
        blk, member, run, rank = (sorting[:, k, :] for k in range(4))
        edge_acc = sorting[:, :, :].rearrange("p a k -> p (a k)")[:, 0:NBANK * BANK]
        count = sb("count", [P, BK])
        total = sb("total", [P, BK])
        totals = sb("totals", [P, BK])[:, :]
        total_i = sb("total_i", [P, BK], I32)
        base = sb("base", [P, BK])
        first_tile = sb("first_tile", [P, BK])
        edge0 = sb("edge0", [P, TCH])
        edge0_i = sb("edge0_i", [P, TCH], I32)
        offset = sb("offset", [P, TCH])
        row_of = sb("row_of", [P, TCH, 2], I32)
        next_dst = sb("next_dst", [P, 1], I32)
        next_blk = sb("next_blk", [P, 1])
        shift = sb("shift", [P, 2, BK])
        disorder = sb("disorder", [P, 1], I32)
        window_out = sb("window_out", [P, SLOTS, 3, P])
        started = member[:, 0:TCH * (BLOCKS - 1)].rearrange("p (c b) -> p c b", c=TCH)
        map_f = sb("map_f", [P, TCH])
        map_i = sb("map_i", [P, 3, TCH], I32)
        pos = sb("pos", [P, TILES], I32)

        slots = sb("slots", [P, TILES, 3])
        gidx = sb("gidx", [P, TILES], I32)
        low = sb("low", [P, TILES])
        weight = sb("weight", [P, TILES])
        src_low = sb("src_low", [P, TILES])
        place = sb("place", [1, 3, TILES], I32)

        x = sb("x", [P, BLOCKS * D])
        r = sb("r", [P, BLOCKS * D])
        spent = slots[:, :, :].rearrange("p k w -> p (k w)")
        y = spent[:, 0:BLOCKS * D]
        dinv = sb("dinv", [P, BLOCKS])
        stat = sb("stat", [P, 4, BLOCKS])
        xT = spent[:, BLOCKS * D:BLOCKS * D + 3 * BANK].rearrange("p (a n) -> p a n", a=3)
        qT = sb("qT", [D, 2, BANK])

        ring = sb("ring", [P, SLOTS, G, ROW])
        hot = sb("hot", [P, SLOTS, G, P])
        h = hot[:, :, :, :].rearrange("p s g e -> p (s g e)")[:, 0:BLOCKS * D]
        idx_ring = sb("idx_ring", [P, SLOTS, G0], I32)
        rec_ring = sb("rec_ring", [P, SLOTS, G0, 3])
        q_now = sb("q_now", [P, 4, D])
        hT = sb("hT", [ROW, 2, P])
        msg = sb("msg", [P, 4, ROW])

        acc = ctx.enter_context(nc.psum_tensor("acc", [P, 8 * BANK], F32))
        spare = acc[:, NBANK * BANK:]

        def bank(k):
            return acc[:, k * BANK:(k + 1) * BANK]

        def by_node(t):
            return t.rearrange("p (k n) -> p k n", n=BANK)[:, :, 0:PER_BANK * ACC]\
                .rearrange("p k (j f) -> p k j f", f=ACC)

        sums = by_node(acc[:, 0:NBANK * BANK])

        def nodes(t):
            return t.rearrange("p (k j f) -> p k j f", k=NBANK, j=PER_BANK)

        def mat(name):
            return mats[:, MATS.index(name), :]

        def bias(name, n):
            i = ROWS.index(name)
            return rows[:, i:i + 1, :].to_broadcast([P, n, D])

        in_dst, in_edges, in_nodes, in_weights = sem("in_dst"), sem("in_edges"), sem("in_nodes"), sem("in_weights")
        fetched = [sem(f"fetched{s}") for s in range(SLOTS)]
        rows_known, window_made, window_turned, window_laid = (
            sem("rows_known"), sem("window_made"), sem("window_turned"), sem("window_laid"))
        window_low_stored = [sem(f"window_low_stored{s}") for s in range(SLOTS)]
        order_known, recs_cleared = sem("order_known"), sem("recs_cleared")
        sent = [sem(f"sent{s}") for s in range(SLOTS)]
        rank_turn = sem("rank_turn")
        dve_sort_step = sem("dve_sort_step")
        iotas, consts, padded, pad_stored = sem("iotas"), sem("consts"), sem("padded"), sem("pad_stored")
        counted, base_sums, map_made, map_stored = (
            sem("counted"), sem("base_sums"), sem("map_made"), sem("map_stored"))
        map_loaded, recs_made, recs_staged = sem("map_loaded"), sem("recs_made"), sem("recs_staged")
        scattered = [sem(f"scattered{s}") for s in range(SLOTS)]
        slots_loaded, derived = sem("slots_loaded"), sem("derived")
        low_turned, low_copied, low_stored = sem("low_turned"), sem("low_copied"), [
            sem(f"low_stored{s}") for s in range(SLOTS)]
        rows_cleared = sem("rows_cleared")
        nodes_ready, turned, turned_out = sem("nodes_ready"), sem("turned"), sem("turned_out")
        q_sums, q_biased, q_ready = sem("q_sums"), sem("q_biased"), sem("q_ready")
        dense_sums, dense_out = sem("dense_sums"), sem("dense_out")
        table_stored = sem("table_stored")
        idx_staged, hot_ready, group_used = sem("idx_staged"), sem("hot_ready"), sem("group_used")
        gathered = [sem(f"gathered{s}") for s in range(SLOTS)]
        low_loaded = [sem(f"low_loaded{s}") for s in range(SLOTS)]
        rows_loaded = [sem(f"rows_loaded{s}") for s in range(SLOTS)]
        deg_summed = sem("deg_summed")
        pos2_made = sem("pos2_made")
        q_copied, edge_sums, edge_hidden = sem("q_copied"), sem("edge_sums"), sem("edge_hidden")
        msg_sums, msg_ready, tile_sums = sem("msg_sums"), sem("msg_ready"), sem("tile_sums")
        tile_added = sem("tile_added")
        root_in, root_out, done, stored = sem("root_in"), sem("root_out"), sem("done"), sem("stored")
        dve_step, act_step, pool_step = sem("dve_step"), sem("act_step"), sem("pool_step")

        CONV1, CONV2, MEAN1, MEAN2, TO_SRC, BY_SRC, EDGE = range(7)
        GATHER_NO = {CONV1: 0, CONV2: 1, MEAN1: 2, MEAN2: 3, EDGE: 4}
        STAGE_NO = {CONV1: 0, CONV2: 1, MEAN1: 2, MEAN2: 3, TO_SRC: 4, EDGE: 5}
        ROOTS = 4 + 2

        def unordered(engine):
            engine.wait_ge(order_known, 1)
            return engine.If(engine.value_load(disorder[0:1, 0:1], min_val=0, max_val=1) > 0)

        block = ctx.enter_context(nc.Block())

        @block.sync
        def _(sp):
            for to, of in ((dst_i, dst_in), (src_i, src_in), (w_raw, w_in)):
                sp.dma_start(to, rectangle(of)).then_inc(in_dst if of is dst_in else in_edges, 16)
            sp.wait_ge(consts, 1)
            with nc.allow_non_contiguous_dma(reason="one number for each partition"):
                sp.dma_start(next_dst[0:P - 1, :],
                             dst_in.rearrange("r e -> (r e)")[COLS:P * COLS]
                             .rearrange("(p j) -> p j", j=COLS)[:, 0:1]).then_inc(in_dst, 16)
            sp.dma_start(mats[:, :, :], mats_in).then_inc(in_weights, 16)
            sp.dma_start(rows[:, :, :], rows_in.partition_broadcast(P)).then_inc(in_weights, 16)
            sp.dma_start(qb[:, :], qb_in).then_inc(in_weights, 16)
            sp.dma_start(bi_stack[0:D, :], mats_in[:, MATS.index("bi1"), :]).then_inc(in_weights, 16)
            sp.dma_start(bi_stack[D:2 * D, :], mats_in[:, MATS.index("bi2"), :]).then_inc(in_weights, 16)
            sp.dma_start(e2[0:D, :], mats_in[:, MATS.index("e2"), :]).then_inc(in_weights, 16)
            sp.dma_start(e2[D:ROW, :], e2b_in).then_inc(in_weights, 16)
            sp.dma_start(x[:, :], x_in).then_inc(in_nodes, 16)
            sp.wait_ge(padded, 1)
            wide_rows = rows_d.rearrange("(p k) w -> p (k w)", p=P)
            one_ring = ring[:, :, :, :].rearrange("p s g w -> p (s g w)")
            for j in range(ROUNDS):
                sp.dma_start(wide_rows[:, j * ROUND * ROW:(j + 1) * ROUND * ROW], one_ring)\
                    .then_inc(rows_cleared, 16)

            def turn_map(n, which):
                sp.wait_ge(map_made, n + 1)
                with nc.allow_non_contiguous_dma(reason="a small table"):
                    for i, m in enumerate(which):
                        sp.dma_start(place_d[m].rearrange("c p -> p c"), map_i[:, m, :])\
                            .then_inc(map_stored, 16)
                    sp.wait_ge(map_stored, 32 if n == 0 else 48)
                for i, m in enumerate(which):
                    sp.dma_start(place[0:1, m, :], place_d[m].rearrange("c p -> (c p)").unsqueeze(0))\
                        .then_inc(map_loaded, 16)

            turn_map(0, (0, 1))
            for c in range(TCH):
                sp.wait_ge(window_made, c + 1)
                sp.dma_start(low_d[c * P:(c + 1) * P, :], window_out[:, c % SLOTS, 1, :])\
                    .then_inc(window_low_stored[c % SLOTS], 16)
            for s in range(SLOTS):
                sp.wait_ge(window_low_stored[s], 16 * -(-(TCH - s) // SLOTS))
            with unordered(sp):
                sp.wait_ge(recs_cleared, 1)
                sp.dma_start(slots_d.rearrange("(p k) w -> p (k w)", p=P),
                             slots[:, :, :].rearrange("p k w -> p (k w)")).then_inc(pad_stored, 16)
                for s in range(SLOTS):
                    sp.wait_ge(scattered[s], ROUNDS0 * G0 * 16)
                sp.dma_start(slots[:, :, :].rearrange("p k w -> p (k w)"),
                             slots_d.rearrange("(p k) w -> p (k w)", p=P)).then_inc(slots_loaded, 16)
                for c in range(TCH):
                    sp.wait_ge(low_copied, c + 1)
                    sp.dma_start(low_d[c * P:(c + 1) * P, :], low_turn[:, c % SLOTS, :])\
                        .then_inc(low_stored[c % SLOTS], 16)
                for s in range(SLOTS):
                    sp.wait_ge(low_stored[s], 16 * -(-(TCH - s) // SLOTS))

            def store_table(layer):
                sp.wait_ge(dense_out, CHUNKS * (layer + 1))
                sp.dma_start(table.rearrange("(p b) f -> p (b f)", p=P), y).then_inc(table_stored, 16)

            store_table(0)
            store_table(1)
            turn_map(1, (2,))
            store_table(2)
            store_table(3)

            def load_low(edge_pass, n):
                with sp.Fori(0, ROUNDS) as i:
                    for s in range(SLOTS):
                        sp.wait_ge(group_used, edge_pass * GROUPS + i * SLOTS + s + 1)
                        sp.dma_start(lowT[:, s, :],
                                     low_d[bass.ds(i * ROUND + s * G, G), :].rearrange("k e -> (k e)")
                                     .partition_broadcast(P)).then_inc(low_loaded[s], 16)

            sp.wait_ge(turned, CHUNKS * 5)
            load_low(TO_SRC, 0)
            for s in range(SLOTS):
                sp.wait_ge(sent[s], ROUNDS * G * 16)
            with sp.Fori(0, ROUNDS) as i:
                for s in range(SLOTS):
                    sp.wait_ge(group_used, BY_SRC * GROUPS + i * SLOTS + s + 1)
                    sp.dma_start(ring[:, s, :, :].rearrange("p g w -> p (g w)"),
                                 wide_rows[:, bass.ds((i * ROUND + s * G) * ROW, G * ROW)])\
                        .then_inc(rows_loaded[s], 16)
            store_table(5)
            load_low(EDGE, 1)
            sp.wait_ge(done, 1)
            sp.dma_start(out, x[:, :]).then_inc(stored, 16)
            sp.wait_ge(stored, 16)
            sp.wait_ge(rows_cleared, 16 * ROUNDS)

        @block.gpsimd
        def _(pool):
            pool.iota(row_iota[:, :], [[1, P]], base=0, channel_multiplier=0,
                      allow_small_or_imprecise_dtypes=True).then_inc(iotas, 1)
            pool.iota(part_iota[:, :], [[1, 1]], base=0, channel_multiplier=1,
                      allow_small_or_imprecise_dtypes=True).then_inc(iotas, 1)
            pool.iota(block_iota[:, :], [[1, BK]], base=0, channel_multiplier=0,
                      allow_small_or_imprecise_dtypes=True).then_inc(iotas, 1)
            pool.iota(tile_iota[:, :], [[P, TCH]], base=0, channel_multiplier=1,
                      allow_small_or_imprecise_dtypes=True).then_inc(iotas, 1)
            pool.wait_ge(rows_known, 1)
            for c in range(TCH):
                if c >= SLOTS:
                    pool.wait_ge(window_made, c - SLOTS + 1)
                for k, of in enumerate((src_in, dst_in, w_in)):
                    for j in range(2):
                        to = hot[:, c % SLOTS, 2 * k + j, :]
                        pool.indirect_dma_start(
                            to if of is w_in else to.bitcast(I32), None, of,
                            bass.IndirectOffsetOnAxis(row_of[:, c, j:j + 1], 0)
                        ).then_inc(fetched[c % SLOTS], 16)
            with unordered(pool):
                pool.wait_ge(pad_stored, 16)
                with pool.Fori(0, ROUNDS0) as i:
                    for s in range(SLOTS):
                        pool.wait_ge(recs_staged, i * SLOTS + s + 1)
                        pool.sem_inc(pool_step, 1)
                        for t in range(G0):
                            pool.indirect_dma_start(
                                slots_d, bass.IndirectOffsetOnAxis(idx_ring[:, s, t:t + 1], 0),
                                rec_ring[:, s, t, :], None, bounds_check=P * TILES - 1, oob_is_err=False
                            ).then_inc(scattered[s], 16)

            def gather(edge_pass, stored_tables):
                pool.wait_ge(table_stored, 16 * stored_tables)
                first = STAGE_NO[edge_pass] * GROUPS
                with pool.Fori(0, ROUNDS) as i:
                    for s in range(SLOTS):
                        pool.wait_ge(idx_staged, first + i * SLOTS + s + 1)
                        pool.sem_inc(pool_step, 1)
                        for t in range(G):
                            pool.indirect_dma_start(
                                ring[:, s, t, 0:D], None, table,
                                bass.IndirectOffsetOnAxis(idx_ring[:, s, t:t + 1], 0)
                            ).then_inc(gathered[s], 16)

            gather(CONV1, 1)
            gather(CONV2, 2)
            gather(MEAN1, 3)
            gather(MEAN2, 4)
            pool.wait_ge(rows_cleared, 16 * ROUNDS)
            first = STAGE_NO[TO_SRC] * GROUPS
            with pool.Fori(0, ROUNDS) as i:
                for s in range(SLOTS):
                    pool.wait_ge(idx_staged, first + i * SLOTS + s + 1)
                    pool.sem_inc(pool_step, 1)
                    for t in range(G):
                        pool.indirect_dma_start(
                            rows_d, bass.IndirectOffsetOnAxis(idx_ring[:, s, t:t + 1], 0),
                            ring[:, s, t, :], None, bounds_check=P * TILES - 1, oob_is_err=False
                        ).then_inc(sent[s], 16)
            gather(EDGE, 5)

        @block.scalar
        def _(act):
            step = Steps(act, act_step)

            def roots(n):
                act.wait_ge(root_in, n + 1)
                nc.scalar.activation(stat[:, 3, :], stat[:, 2, :], ACT.Sqrt).then_inc(root_out, 1)

            for c in range(TCH):
                act.wait_ge(window_turned, c + 1)
                nc.scalar.copy(slots[:, c * P:(c + 1) * P, :],
                               bank(c % 4)[:, 0:3 * P].rearrange("p (w k) -> p k w", w=3))\
                    .then_inc(window_laid, 1)

            with unordered(act):
                act.wait_ge(recs_made, 1)

                def stage_records(i, waits):
                    for s in range(SLOTS):
                        at = i * SLOTS * G0 + s * G0
                        if waits:
                            act.wait_ge(scattered[s], i * (G0 * 16))
                        nc.scalar.copy(idx_ring[:, s, :], pos[:, bass.ds(at, G0)])
                        nc.scalar.copy(rec_ring[:, s, :, :], slots[:, bass.ds(at, G0), :])\
                            .then_inc(recs_staged, 1)

                stage_records(0, False)
                with act.Fori(1, ROUNDS0) as i:
                    stage_records(i, True)
                for c in range(TCH):
                    act.wait_ge(low_turned, c + 1)
                    if c >= SLOTS:
                        act.wait_ge(low_stored[c % SLOTS], 16 * (c // SLOTS))
                    nc.scalar.copy(low_turn[:, c % SLOTS, :], bank(c % 4)[:, 0:P]).then_inc(low_copied, 1)

            def dense(layer):
                mid = layer in (2, 3)
                width = 2 * D if layer == 4 else D
                for c in range(CHUNKS + 1):
                    n = layer * CHUNKS + c
                    if c < CHUNKS:
                        cols = min(CH, BLOCKS - CH * c) * P
                        act.wait_ge(turned, n + 1)
                        if n >= 3:
                            act.wait_ge(dense_sums, n - 2)
                        nc.scalar.copy(xT[0:width, n % 3, 0:cols], bank(n % 2)[0:width, 0:cols])\
                            .then_inc(turned_out, 1)
                    if mid and c >= 1:
                        cols = min(CH, BLOCKS - CH * (c - 1)) * P
                        q = (layer - 2) * CHUNKS + c - 1
                        act.wait_ge(q_sums, q + 1)
                        if c >= 3:
                            act.wait_ge(dense_sums, n - 2)
                        nc.scalar.activation(qT[:, q % 2, 0:cols], bank(2 + q % 2)[0:D, 0:cols],
                                             ACT.Identity, bias=qb[:, layer - 2:layer - 1])\
                            .then_inc(q_biased, 1)

            def stage_indices(edge_pass):
                with act.Fori(0, ROUNDS) as i:
                    for s in range(SLOTS):
                        act.wait_ge(group_used, edge_pass * GROUPS + i * SLOTS + s + 1)
                        nc.scalar.copy(idx_ring[:, s, 0:G], gidx[:, bass.ds(i * ROUND + s * G, G)])\
                            .then_inc(idx_staged, 1)

            dense(0)
            stage_indices(CONV1)
            dense(1)
            stage_indices(CONV2)
            roots(0)
            dense(2)
            stage_indices(MEAN1)
            roots(1)
            dense(3)
            stage_indices(MEAN2)
            roots(2)
            roots(3)
            act.wait_ge(root_in, 5)
            nc.scalar.activation(stat[:, 3, :], stat[:, 2, :], ACT.Sqrt).then_inc(root_out, 1)
            dense(4)
            act.wait_ge(pos2_made, 1)

            def send_rows(i, waits):
                for s in range(SLOTS):
                    at = i * ROUND + s * G
                    act.wait_ge(group_used, SLOTS + TO_SRC * GROUPS + i * SLOTS + s + 1)
                    if waits:
                        act.wait_ge(sent[s], i * (G * 16))
                    nc.scalar.copy(ring[:, s, :, 0:D], bank(s).rearrange("p (g f) -> p g f", g=G))
                    nc.scalar.copy(ring[:, s, :, D:ROW], src_low[:, bass.ds(at, G)].unsqueeze(2))
                    nc.scalar.copy(idx_ring[:, s, 0:G], pos[:, bass.ds(at, G)]).then_inc(idx_staged, 1)

            send_rows(0, False)
            with act.Fori(1, ROUNDS) as i:
                send_rows(i, True)
            roots(5)
            dense(5)
            AHEAD = SLOTS - 1

            def edge_indices(n, at):
                act.wait_ge(group_used, EDGE * GROUPS + n + 1)
                nc.scalar.copy(idx_ring[:, at % SLOTS, 0:G], gidx[:, bass.ds(n * G, G)])\
                    .then_inc(idx_staged, 1)

            def edge_round(i, last):
                for s in range(SLOTS):
                    if not last or s + AHEAD < SLOTS:
                        edge_indices(i * SLOTS + s + AHEAD, s + AHEAD)
                    at = i * ROUND + s * G
                    _, of = nc.values_load_multi_w_load_instructions(
                        place[0:1, 1, bass.ds(at, G)], engines=(ACT_ENGINE,), min_val=0,
                        max_val=(BLOCKS - 1) * D, skip_runtime_bounds_check_because="counted blocks")

                    def copy_q(t):
                        if t >= 4:
                            act.wait_ge(edge_sums, at + t - 3)
                        nc.scalar.copy(q_now[:, t % 4, :], r[:, bass.ds(of[t], D)]).then_inc(q_copied, 1)

                    for t in range(3):
                        copy_q(t)
                    for t in range(G):
                        if t + 3 < G:
                            copy_q(t + 3)
                        act.wait_ge(edge_sums, at + t + 1)
                        if t >= 2:
                            act.wait_ge(msg_sums, at + t - 1)
                        nc.scalar.activation(hT[0:D, t % 2, :], bank(t % 2)[0:D, 0:P],
                                             ACT.Relu).then_inc(edge_hidden, 1)

            for n in range(AHEAD):
                edge_indices(n, n)
            act.wait_ge(dense_out, CHUNKS * LAYERS)
            with act.Fori(0, ROUNDS - 1) as i:
                edge_round(i, False)
            edge_round(ROUNDS - 1, True)
            roots(6)

        @block.vector
        def _(dve):
            step = Steps(dve, dve_step)
            v = nc.vector

            dve.sem_inc(tile_added, 2)
            v.memset(next_dst[:, :], PAD_NODE)
            v.memset(zeros[:, :], 0.0).then_inc(consts, 1)
            dve.wait_ge(iotas, 4)
            v.memset(ones[:, :], 1.0).then_inc(consts, 1)
            v.tensor_scalar(ident[:, :], row_iota[:, :], part_iota[:, :], None, ALU.is_equal)\
                .then_inc(consts, 1)
            v.tensor_scalar(before[:, :], row_iota[:, :], part_iota[:, :], None, ALU.is_gt)\
                .then_inc(consts, 1)
            v.memset(hT[D:ROW, :, :], 1.0).then_inc(consts, 1)
            v.memset(msg[:, :, :], 1.0).then_inc(consts, 1)
            step(v.memset(ring[:, :, :, 0:D], 0.0))
            v.memset(ring[:, :, :, D:ROW], PAD_LOW).then_inc(padded, 1)

            def count_block(b, cols):
                step(v.tensor_scalar(member[:, 0:cols], blk[:, 0:cols], block_iota[:, bass.ds(b, 1)],
                                     None, ALU.is_equal, ALU.add, accum_out=count[:, bass.ds(b, 1)]))

            COUNT_STEPS = 1

            def rank_block(step, b, cols):
                step(v.tensor_scalar(member[:, 0:cols], blk[:, 0:cols], block_iota[:, bass.ds(b, 1)],
                                     None, ALU.is_equal))
                step(v.tensor_tensor_scan(run[:, 0:cols], member[:, 0:cols], member[:, 0:cols],
                                          base[:, bass.ds(b, 1)], ALU.add, ALU.max))
                dve.sem_inc(rank_turn, 1)
                step(v.copy_predicated(rank[:, 0:cols], member[:, 0:cols].bitcast(I32), run[:, 0:cols]))

            RANK_STEPS = 3

            def bases(n):
                v.engine_nop().then_inc(counted, 1)
                dve.wait_ge(base_sums, n + 1)
                step(v.tensor_copy(totals, spare[:, 64:64 + BK]))
                step(v.tensor_scalar(total[:, :], totals, float(P - 1), None, ALU.add))
                step(v.tensor_copy(total_i[:, :], total[:, :]))
                step(v.tensor_scalar(total_i[:, :], total_i[:, :], 7, None, ALU.arith_shift_right))
                step(v.tensor_copy(total[:, :], total_i[:, :]))
                step(v.tensor_tensor_scan(first_tile[:, :], total[:, :], total[:, :], 0.0, ALU.add, ALU.max))
                step(v.tensor_tensor(first_tile[:, :], first_tile[:, :], total[:, :], ALU.subtract))
                step(v.scalar_tensor_tensor(base[:, :], first_tile[:, :], float(P), spare[:, 0:BK],
                                            ALU.mult, ALU.add))
                step(v.tensor_tensor(
                    started, tile_iota[:, :].unsqueeze(2).to_broadcast([P, TCH, BLOCKS - 1]),
                    first_tile[:, None, 1:BLOCKS].to_broadcast([P, TCH, BLOCKS - 1]), ALU.is_ge))
                step(v.tensor_reduce(map_f[:, :], started, AX.X, ALU.add))
                m = 1 if n == 0 else 2
                step(v.tensor_scalar(map_i[:, m, :], map_f[:, :], float(D), None, ALU.mult))
                to = 0 if n == 0 else 2
                step(v.tensor_scalar(total_i[:, 0:TCH], map_f[:, :], 37.0, None, ALU.mult))
                step(v.tensor_scalar(total_i[:, 0:TCH], total_i[:, 0:TCH], 8, None, ALU.arith_shift_right))
                step(v.tensor_copy(total[:, 0:TCH], total_i[:, 0:TCH]))
                step(v.tensor_scalar(total[:, 0:TCH], total[:, 0:TCH], float(BANK - PER_BANK * ACC), None,
                                     ALU.mult))
                v.scalar_tensor_tensor(map_i[:, to, :], map_f[:, :], float(ACC), total[:, 0:TCH],
                                       ALU.mult, ALU.add).then_inc(map_made, 1)

            def slot_numbers(step, cols):
                step(v.tensor_scalar(rank[:, 0:cols], rank[:, 0:cols], -1.0, None, ALU.add))
                step(v.tensor_copy(member[:, 0:cols].bitcast(I32), rank[:, 0:cols]))
                step(v.tensor_scalar(pos[:, 0:cols], member[:, 0:cols].bitcast(I32), P - 1, None,
                                     ALU.bitwise_and))
                step(v.tensor_copy(rank[:, 0:cols], pos[:, 0:cols]))
                step(v.tensor_scalar(pos[:, 0:cols], member[:, 0:cols].bitcast(I32), 7, None,
                                     ALU.arith_shift_right))
                step(v.tensor_copy(run[:, 0:cols], pos[:, 0:cols]))
                step(v.scalar_tensor_tensor(run[:, 0:cols], rank[:, 0:cols], float(TILES), run[:, 0:cols],
                                            ALU.mult, ALU.add))
                step(v.tensor_scalar(rank[:, 0:cols], blk[:, 0:cols], float(BLOCKS), 1e6, ALU.is_ge,
                                     ALU.mult))
                return v.tensor_tensor(pos[:, 0:cols], run[:, 0:cols], rank[:, 0:cols], ALU.add)

            dve.wait_ge(in_dst, 32)
            step(v.memset(count[:, :], 0.0))
            step(v.tensor_scalar(pos[:, 0:COLS], dst_i, 7, None, ALU.arith_shift_right))
            step(v.tensor_copy(blk[:, 0:COLS], pos[:, 0:COLS]))
            step(v.tensor_scalar(next_dst[:, :], next_dst[:, :], 7, None, ALU.arith_shift_right))
            step(v.tensor_copy(next_blk[:, :], next_dst[:, :]))
            step(v.tensor_tensor(member[:, 0:COLS - 1], blk[:, 1:COLS], blk[:, 0:COLS - 1], ALU.is_lt))
            step(v.tensor_tensor(member[:, COLS - 1:COLS], next_blk[:, :], blk[:, COLS - 1:COLS], ALU.is_lt))
            step(v.tensor_reduce(count[:, BLOCKS:BLOCKS + 1], member[:, 0:COLS], AX.X, ALU.add))
            step.loop(BLOCKS, COUNT_STEPS, lambda b: count_block(b, COLS))
            bases(0)
            starts, grows = shift[:, 0, :], shift[:, 1, :]
            step(v.tensor_tensor_scan(starts, totals, totals, 0.0, ALU.add, ALU.max))
            step(v.tensor_tensor(starts, starts, totals, ALU.subtract))
            step(v.scalar_tensor_tensor(starts, first_tile[:, :], -float(P), starts, ALU.mult, ALU.add))
            step(v.tensor_tensor(grows[:, 1:BLOCKS], starts[:, 1:BLOCKS], starts[:, 0:BLOCKS - 1],
                                 ALU.subtract))
            step(v.tensor_tensor(started, started,
                                 shift[:, 1:2, 1:BLOCKS].to_broadcast([P, TCH, BLOCKS - 1]), ALU.mult))
            step(v.tensor_reduce(edge0[:, :], started, AX.X, ALU.add))
            step(v.scalar_tensor_tensor(edge0[:, :], tile_iota[:, :], float(P), edge0[:, :],
                                        ALU.mult, ALU.add))
            step(v.tensor_copy(edge0_i[:, :], edge0[:, :]))
            step(v.tensor_scalar(row_of[:, :, 0], edge0_i[:, :], 7, None, ALU.arith_shift_right))
            step(v.tensor_copy(edge0[:, :], row_of[:, :, 0]))
            step(v.tensor_scalar(edge0_i[:, :], edge0_i[:, :], P - 1, None, ALU.bitwise_and))
            step(v.tensor_copy(offset[:, :], edge0_i[:, :]))
            v.tensor_scalar(row_of[:, :, 1], edge0[:, :], 1.0, None, ALU.add).then_inc(rows_known, 1)
            for c in range(TCH):
                s = c % SLOTS
                part = [hot[:, s, j, :] for j in range(G)]
                src2, dst2, w2, mask, wrong = part[1], part[3], part[5], part[6], part[7]
                o_src, o_low, o_w = (window_out[:, s, k, :] for k in range(3))
                dve.wait_ge(fetched[s], 96 * (c // SLOTS + 1))
                step(v.tensor_scalar(mask, row_iota[:, :], offset[:, c:c + 1], None, ALU.is_ge))
                if c >= SLOTS:
                    dve.wait_ge(window_turned, c - SLOTS + 1)
                    dve.wait_ge(window_low_stored[s], 16 * (c // SLOTS))
                v.copy_predicated(src2, mask.bitcast(I32), part[0])
                v.copy_predicated(w2, mask.bitcast(I32), part[4])
                step(v.copy_predicated(dst2, mask.bitcast(I32), part[2]))
                v.tensor_copy(o_src, src2.bitcast(I32))
                v.tensor_copy(o_w, w2)
                v.tensor_scalar(part[2].bitcast(I32), dst2.bitcast(I32), 7, None, ALU.arith_shift_right)
                step(v.tensor_scalar(part[0].bitcast(I32), dst2.bitcast(I32), P - 1, None, ALU.bitwise_and))
                step(v.tensor_scalar(wrong, part[2].bitcast(I32), map_f[:, c:c + 1], None, ALU.not_equal))
                v.scalar_tensor_tensor(o_src, wrong, float(PAD_NODE), o_src, ALU.mult, ALU.max)
                v.scalar_tensor_tensor(o_low, wrong, PAD_LOW, part[0].bitcast(I32), ALU.mult, ALU.max)\
                    .then_inc(window_made, 1)
            step(v.tensor_scalar(shift[:, 0, 0:1], totals[:, BLOCKS:BLOCKS + 1], 1.0, None, ALU.min))
            v.tensor_copy(disorder[:, :], shift[:, 0, 0:1]).then_inc(order_known, 1)
            dve.wait_ge(window_laid, TCH)
            with unordered(dve):
                sort_step = Steps(dve, dve_sort_step)
                dve.wait_ge(in_edges, 32)
                v.memset(slots[:, :, 0:1], float(PAD_NODE))
                v.memset(slots[:, :, 1:2], PAD_LOW)
                v.memset(slots[:, :, 2:3], 0.0).then_inc(recs_cleared, 1)
                sort_step(v.memset(rank[:, :], 0.0))
                sort_step.loop(BLOCKS, RANK_STEPS, lambda b: rank_block(sort_step, b, COLS))
                sort_step(slot_numbers(sort_step, COLS))
                dve.wait_ge(pad_stored, 16)
                sort_step(v.tensor_scalar(member[:, 0:COLS].bitcast(I32), dst_i, P - 1, None,
                                          ALU.bitwise_and))
                v.tensor_copy(slots[:, 0:COLS, 0:1], src_i.unsqueeze(2))
                v.tensor_copy(slots[:, 0:COLS, 1:2], member[:, 0:COLS].bitcast(I32).unsqueeze(2))
                v.tensor_copy(slots[:, 0:COLS, 2:3], w_raw.unsqueeze(2)).then_inc(recs_made, 1)
                dve.wait_ge(slots_loaded, 16)
                dve.wait_ge(low_copied, TCH)
            dve.wait_ge(rows_cleared, 16 * ROUNDS)
            step(v.memset(ring[:, :, :, D:ROW], 1.0))

            v.tensor_copy(low[:, :], slots[:, :, 1])
            v.tensor_copy(weight[:, :], slots[:, :, 2])
            step(v.tensor_copy(pos[:, :], slots[:, :, 0]))
            step(v.tensor_scalar(gidx[:, :], pos[:, :], P - 1, None, ALU.bitwise_and))
            step(v.tensor_copy(src_low[:, :], gidx[:, :]))
            step(v.tensor_scalar(gidx[:, :], pos[:, :], 7, None, ALU.arith_shift_right))
            step(v.tensor_copy(blk[:, :], gidx[:, :]))
            step(v.scalar_tensor_tensor(member[:, :], src_low[:, :], float(BLOCKS), blk[:, :],
                                        ALU.mult, ALU.add))
            v.tensor_scalar(gidx[:, :], member[:, :], float(P * BLOCKS - 1), None, ALU.min)\
                .then_inc(derived, 1)
            step(v.memset(count[:, :], 0.0))
            step(v.memset(rank[:, :], 0.0))

            def dense(layer):
                mid = layer in (2, 3)
                for c in range(CHUNKS + 1):
                    if mid and c < CHUNKS:
                        cols = min(CH, BLOCKS - CH * c) * P
                        q = (layer - 2) * CHUNKS + c
                        dve.wait_ge(q_biased, q + 1)
                        v.scalar_tensor_tensor(qT[:, q % 2, 0:cols], qT[:, q % 2, 0:cols], SLOPE,
                                               qT[:, q % 2, 0:cols], ALU.mult, ALU.max).then_inc(q_ready, 1)
                    if c >= 1:
                        b0, n = CH * (c - 1), min(CH, BLOCKS - CH * (c - 1))
                        dve.wait_ge(dense_sums, layer * CHUNKS + c)
                        both = bank(4 + (layer * CHUNKS + c - 1) % 2)[:, 0:n * P]\
                            .rearrange("p (b w) -> p b w", b=n)
                        yv = y[:, b0 * D:(b0 + n) * D].rearrange("p (b f) -> p b f", b=n)
                        rv = r[:, b0 * D:(b0 + n) * D].rearrange("p (b f) -> p b f", b=n)
                        if layer == 4:
                            v.tensor_tensor(yv, both[:, :, 0:D],
                                            dinv[:, b0:b0 + n].unsqueeze(2).to_broadcast([P, n, D]), ALU.mult)
                            step(v.tensor_tensor(rv, both[:, :, D:], bias("bi1", n), ALU.add))
                            v.tensor_tensor(rv, rv, bias("bi2", n), ALU.add).then_inc(dense_out, 1)
                        else:
                            v.tensor_copy(yv, both[:, :, 0:D])
                            name = {0: "c1", 1: "c2", 2: "w0", 3: "w1", 5: "e1"}[layer]
                            v.tensor_tensor(rv, both[:, :, D:], bias(name, n), ALU.add)\
                                .then_inc(dense_out, 1)

            def hots(s, at, numbers, weighted):
                ins = v.tensor_tensor(
                    hot[:, s, :, :], row_iota[:, None, :].to_broadcast([P, G, P]),
                    numbers.unsqueeze(2).to_broadcast([P, G, P]), ALU.is_equal)
                if weighted:
                    step(ins)
                    ins = v.tensor_tensor(
                        hot[:, s, :, :], hot[:, s, :, :],
                        weight[:, bass.ds(at, G)].unsqueeze(2).to_broadcast([P, G, P]), ALU.mult)
                return ins

            def convolve(edge_pass, weighted=False, more=None, more_steps=0):
                each = more_steps + (SLOTS if weighted else 0)

                def body(i):
                    for s in range(SLOTS):
                        at = i * ROUND + s * G
                        dve.wait_ge(group_used, edge_pass * GROUPS + i * SLOTS + s + 1)
                        if edge_pass == CONV2:
                            v.tensor_tensor(
                                src_hot[:, s, :, :], row_iota[:, None, :].to_broadcast([P, G, P]),
                                src_low[:, bass.ds(at, G)].unsqueeze(2).to_broadcast([P, G, P]),
                                ALU.is_equal)
                            v.tensor_tensor(
                                src_blk[:, s, :, :],
                                block_iota[:, None, 0:BLOCKS].to_broadcast([P, G, BLOCKS]),
                                blk[:, bass.ds(at, G)].unsqueeze(2).to_broadcast([P, G, BLOCKS]),
                                ALU.is_equal)
                        hots(s, at, low[:, bass.ds(at, G)], weighted).then_inc(hot_ready, 1)
                    if more is not None:
                        more(i)

                step.loop(ROUNDS, each, body)
                dve.wait_ge(group_used, SLOTS + (edge_pass + 1) * GROUPS)

            def relu_sums():
                step(v.tensor_tensor(nodes(h), sums[:, :, :, 0:D], nodes(r[:, :]), ALU.add))
                step(v.tensor_scalar(h, h, 0.0, None, ALU.max))

            def column(t, k):
                return t[:, k, :].rearrange("p (k j) -> p k j", k=NBANK)

            def wide_stat(k):
                return column(stat, k).unsqueeze(3).to_broadcast([P, NBANK, PER_BANK, D])

            def row_sums(of, to):
                step(v.tensor_reduce(column(stat, to), of, AX.X, ALU.add))

            def root(n):
                v.engine_nop().then_inc(root_in, 1)
                dve.wait_ge(root_out, n + 1)

            def layer_norm(n):
                step(v.tensor_tensor(x[:, :], x[:, :], h, ALU.add))
                row_sums(nodes(x[:, :]), 0)
                step(v.tensor_scalar(stat[:, 0, :], stat[:, 0, :], 1.0 / D, None, ALU.mult))
                step(v.tensor_tensor(nodes(x[:, :]), nodes(x[:, :]), wide_stat(0), ALU.subtract))
                step(v.tensor_tensor(h, x[:, :], x[:, :], ALU.mult))
                row_sums(nodes(h), 1)
                step(v.tensor_scalar(stat[:, 2, :], stat[:, 1, :], 1.0 / D, EPS, ALU.mult, ALU.add))
                root(n)
                step(v.reciprocal(stat[:, 0, :], stat[:, 3, :]))
                step(v.tensor_tensor(nodes(x[:, :]), nodes(x[:, :]), wide_stat(0), ALU.mult))

            def mean_norm(n):
                wsum = sums[:, :, :, D]
                step(v.tensor_scalar(column(stat, 0), wsum, 0.0, None, ALU.is_equal))
                step(v.tensor_tensor(column(stat, 0), column(stat, 0), wsum, ALU.add))
                step(v.reciprocal(stat[:, 1, :], stat[:, 0, :]))
                step(v.tensor_tensor(nodes(h), sums[:, :, :, 0:D], wide_stat(1), ALU.mult))
                step(v.tensor_tensor(h, h, r[:, :], ALU.add))
                step(v.scalar_tensor_tensor(h, h, SLOPE, h, ALU.mult, ALU.max))
                step(v.tensor_tensor(r[:, :], h, h, ALU.mult))
                row_sums(nodes(r[:, :]), 2)
                root(n)
                step(v.tensor_scalar(stat[:, 0, :], stat[:, 3, :], 0.0, None, ALU.is_equal))
                step(v.tensor_tensor(stat[:, 0, :], stat[:, 0, :], stat[:, 3, :], ALU.add))
                step(v.reciprocal(stat[:, 1, :], stat[:, 0, :]))
                step(v.tensor_tensor(nodes(h), nodes(h), wide_stat(1), ALU.mult))

            def ready():
                v.engine_nop().then_inc(nodes_ready, 1)

            dve.wait_ge(in_weights, 16 * 7)
            v.tensor_tensor(edge_w[:, 0, :], mat("e1a"), mat("e1b"), ALU.subtract)
            step(v.tensor_copy(edge_w[:, 1, :], mat("e1b")))
            dve.wait_ge(in_nodes, 16)
            ready()
            dense(0)
            convolve(CONV1, more=lambda i: count_block(i, TILES), more_steps=COUNT_STEPS)
            relu_sums()
            ready()
            dense(1)
            bases(1)
            convolve(CONV2, more=lambda i: rank_block(step, i, TILES), more_steps=RANK_STEPS)
            dve.wait_ge(deg_summed, 1)
            step(v.tensor_copy(dinv[:, :], spare[:, 128:128 + BLOCKS]))
            step(slot_numbers(step, TILES))
            v.engine_nop().then_inc(pos2_made, 1)
            relu_sums()
            layer_norm(0)
            ready()
            dense(2)
            convolve(MEAN1, weighted=True)
            mean_norm(1)
            ready()
            dense(3)
            convolve(MEAN2, weighted=True)
            mean_norm(2)
            layer_norm(3)
            step(v.tensor_scalar(stat[:, 2, :], dinv[:, :], 1.0, None, ALU.max))
            root(4)
            step(v.reciprocal(stat[:, 0, :], stat[:, 3, :]))
            step(v.tensor_scalar(stat[:, 1, :], dinv[:, :], 0.0, None, ALU.is_gt))
            step(v.tensor_tensor(dinv[:, :], stat[:, 0, :], stat[:, 1, :], ALU.mult))
            xb = x[:, :].rearrange("p (b f) -> p b f", b=BLOCKS)
            v.tensor_copy(pairs[:, :, 0:D], xb)
            step(v.tensor_tensor(pairs[:, :, D:], xb, xb, ALU.mult))
            ready()
            dense(4)

            def turned_hots(n, i, s):
                dve.wait_ge(low_loaded[s], (n * ROUNDS + i + 1) * 16)
                return v.tensor_scalar(hotT[:, s, :], lowT[:, s, :], part_iota[:, :], None, ALU.is_equal)

            with dve.Fori(0, ROUNDS) as i:
                for s in range(SLOTS):
                    turned_hots(0, i, s).then_inc(hot_ready, 1)
            with dve.Fori(0, ROUNDS) as i:
                for s in range(SLOTS):
                    dve.wait_ge(rows_loaded[s], (i + 1) * 16)
                    dve.wait_ge(group_used, BY_SRC * GROUPS + i * SLOTS + s + 1)
                    hots(s, None, ring[:, s, :, D], False).then_inc(hot_ready, 1)
            dve.wait_ge(group_used, SLOTS + (BY_SRC + 1) * GROUPS)
            db = dinv[:, :].rearrange("p (k j) -> p k j", k=NBANK).unsqueeze(3)\
                .to_broadcast([P, NBANK, PER_BANK, D])
            step(v.tensor_tensor(nodes(h), sums[:, :, :, 0:D], db, ALU.mult))
            step(v.tensor_tensor(h, h, r[:, :], ALU.add))
            layer_norm(5)
            ready()
            dense(5)
            first = EDGE * GROUPS
            step(v.memset(edge_acc, 0.0))

            def edge_hots(i, s):
                dve.wait_ge(group_used, first + i * SLOTS + s + 1)
                turned_hots(1, i, s)
                hots(s, None, low[:, bass.ds(i * ROUND + s * G, G)], False).then_inc(hot_ready, 1)

            def messages(i, s):
                at = i * ROUND + s * G
                _, to = nc.values_load_multi_w_load_instructions(
                    place[0:1, 0, bass.ds(at, G)], engines=(DVE_ENGINE,), min_val=0, max_val=LAST_PLACE,
                    skip_runtime_bounds_check_because="counted blocks")
                for t in range(G + 1):
                    if t < G:
                        dve.wait_ge(msg_sums, at + t + 1)
                        v.tensor_scalar(msg[:, t % 4, 0:D], bank(2 + t % 2)[:, 0:D], 0.0,
                                        None, ALU.max).then_inc(msg_ready, 1)
                    if t >= 1:
                        dve.wait_ge(tile_sums, at + t)
                        here = edge_acc[:, bass.ds(to[t - 1], ROW)]
                        v.tensor_tensor(here, here, bank(4 + (t - 1) % 2)[:, 0:ROW], ALU.add)\
                            .then_inc(tile_added, 1)
                        dve.wait_ge(tile_added, at + t + 2)

            def edge_round(i, last):
                for s in range(SLOTS):
                    if s + 1 < SLOTS:
                        edge_hots(i, s + 1)
                    elif not last:
                        edge_hots(i + 1, 0)
                    messages(i, s)

            edge_hots(0, 0)
            with dve.Fori(0, ROUNDS - 1) as i:
                edge_round(i, False)
            edge_round(ROUNDS - 1, True)
            edge_sums_by_node = by_node(edge_acc)
            step(v.tensor_scalar(column(stat, 0), edge_sums_by_node[:, :, :, D], 1.0, None, ALU.max))
            step(v.reciprocal(stat[:, 1, :], stat[:, 0, :]))
            step(v.tensor_tensor(nodes(h), edge_sums_by_node[:, :, :, 0:D], wide_stat(1), ALU.mult))
            layer_norm(6)
            v.engine_nop().then_inc(done, 1)

        @block.tensor
        def _(pe):
            mm = nc.tensor.matmul
            pe.sem_inc(group_used, SLOTS)
            pe.wait_ge(consts, 6)

            def base_products(n):
                pe.wait_ge(counted, n + 1)
                mm(spare[:, 0:BK], before[:, :], count[:, :], start=True, stop=True)
                mm(spare[:, 64:64 + BK], ones[:, :], count[:, :], start=True, stop=True)\
                    .then_inc(base_sums, 1)

            base_products(0)
            for c in range(TCH):
                pe.wait_ge(window_made, c + 1)
                if c >= 4:
                    pe.wait_ge(window_laid, c - 3)
                for k in range(3):
                    last = mm(bank(c % 4)[:, k * P:(k + 1) * P], window_out[:, c % SLOTS, k, :], ident[:, :],
                              start=True, stop=True)
                last.then_inc(window_turned, 1)
            pe.wait_ge(window_laid, TCH)
            with unordered(pe):
                pe.wait_ge(slots_loaded, 16)
                for c in range(TCH):
                    if c >= 4:
                        pe.wait_ge(low_copied, c - 3)
                    mm(bank(c % 4)[:, 0:P], slots[:, c * P:(c + 1) * P, 1], ident[:, :],
                       start=True, stop=True).then_inc(low_turned, 1)
                pe.wait_ge(low_copied, TCH)
            pe.wait_ge(in_weights, 16 * 7)
            pe.wait_ge(map_loaded, 32)

            def dense(layer, source):
                mid = layer in (2, 3)
                width = 2 * D if layer == 4 else D
                lag = 2 if mid else 1
                pe.wait_ge(nodes_ready, layer + 1)
                for c in range(CHUNKS + lag):
                    n = layer * CHUNKS + c
                    if c < CHUNKS:
                        if n >= 2:
                            pe.wait_ge(turned_out, n - 1)
                        for t in range(min(CH, BLOCKS - CH * c)):
                            b = CH * c + t
                            last = mm(bank(n % 2)[0:width, t * P:(t + 1) * P],
                                      source[:, b * width:(b + 1) * width], ident[:, :],
                                      start=True, stop=True)
                        last.then_inc(turned, 1)
                    if mid and 1 <= c <= CHUNKS:
                        q = (layer - 2) * CHUNKS + c - 1
                        cols = min(CH, BLOCKS - CH * (c - 1)) * P
                        pe.wait_ge(turned_out, n)
                        if q >= 2:
                            pe.wait_ge(q_biased, q - 1)
                        mm(bank(2 + q % 2)[0:D, 0:cols], mat("q0" if layer == 2 else "q1"),
                           xT[0:D, (n - 1) % 3, 0:cols], start=True, stop=True).then_inc(q_sums, 1)
                    if c >= lag:
                        m = n - lag
                        pe.wait_ge(turned_out, m + 1)
                        if mid:
                            q = (layer - 2) * CHUNKS + c - lag
                            pe.wait_ge(q_ready, q + 1)
                        if m >= 2:
                            pe.wait_ge(dense_out, m - 1)
                        for t in range(min(CH, BLOCKS - CH * (c - lag))):
                            tile = slice(t * P, (t + 1) * P)
                            own = xT[0:D, m % 3, tile]
                            left, right = bank(4 + m % 2)[:, t * P:t * P + D], \
                                bank(4 + m % 2)[:, t * P + D:(t + 1) * P]
                            if layer < 2:
                                a, b = ("c1_rel", "c1_root") if layer == 0 else ("c2_rel", "c2_root")
                                pairs_of = (own, mat(a)), (own, mat(b))
                            elif mid:
                                k = layer - 2
                                pairs_of = (qT[:, q % 2, tile], mat(f"wb{k}")), (own, mat(f"wa{k}"))
                            elif layer == 4:
                                pairs_of = (xT[:, m % 3, tile], bi_stack[:, :]), (own, mat("bi1"))
                            else:
                                pairs_of = (own, edge_w[:, 0, :]), (own, edge_w[:, 1, :])
                            mm(left, *pairs_of[0], start=True, stop=True)
                            last = mm(right, *pairs_of[1], start=True, stop=True)
                        last.then_inc(dense_sums, 1)
                pe.wait_ge(dense_out, (layer + 1) * CHUNKS)

            def clear_sums(times=1):
                for _ in range(times):
                    for k in range(NBANK):
                        mm(bank(k), zeros[:, 0:P], zeros[:, :], start=True, stop=True)

            def blocks_of(which, at):
                _, values = nc.values_load_multi_w_load_instructions(
                    place[0:1, which, bass.ds(at, G)], engines=(PE_ENGINE,), min_val=0,
                    max_val=(BLOCKS - 1) * D if which == 1 else LAST_PLACE,
                    skip_runtime_bounds_check_because="counted blocks")
                return values

            def convolve(edge_pass):
                if edge_pass == BY_SRC:
                    pe.wait_ge(hot_ready, BY_SRC * GROUPS + 1)
                clear_sums(3 if edge_pass == BY_SRC else 1)
                if edge_pass == CONV2:
                    mm(spare[:, 128:128 + BLOCKS], zeros[:, 0:P], zeros[:, 0:BLOCKS], start=True, stop=True)
                columns = ROW if edge_pass in (MEAN1, MEAN2) else D
                with pe.Fori(0, ROUNDS) as i:
                    for s in range(SLOTS):
                        at = i * ROUND + s * G
                        to = blocks_of(2 if edge_pass == BY_SRC else 0, at)
                        pe.wait_ge(hot_ready, edge_pass * GROUPS + i * SLOTS + s + 1)
                        if edge_pass != BY_SRC:
                            pe.wait_ge(gathered[s], (GATHER_NO[edge_pass] * ROUNDS + i + 1) * (G * 16))
                        for t in range(G):
                            if edge_pass == CONV2:
                                mm(spare[:, 128:128 + BLOCKS], src_hot[:, s, t, :], src_blk[:, s, t, :],
                                   start=False, stop=True, skip_group_check=True)
                            last = mm(acc[:, bass.ds(to[t], columns)], hot[:, s, t, :],
                                      ring[:, s, t, 0:columns],
                                      start=False, stop=True, skip_group_check=True)
                        last.then_inc(group_used, 1)

            dense(0, x)
            convolve(CONV1)
            dense(1, h)
            base_products(1)
            pe.wait_ge(map_made, 2)
            convolve(CONV2)
            mm(spare[:, 64:65], zeros[:, 0:P], zeros[:, 0:1], start=True, stop=True).then_inc(deg_summed, 1)
            dense(2, x)
            convolve(MEAN1)
            dense(3, h)
            convolve(MEAN2)
            dense(4, wide)
            with pe.Fori(0, ROUNDS) as i:
                for s in range(SLOTS):
                    of = blocks_of(1, i * ROUND + s * G)
                    pe.wait_ge(hot_ready, TO_SRC * GROUPS + i * SLOTS + s + 1)
                    pe.wait_ge(idx_staged, STAGE_NO[TO_SRC] * GROUPS + i * SLOTS + s + 1 - SLOTS)
                    for t in range(G):
                        last = mm(bank(s)[:, t * D:(t + 1) * D], hotT[:, s, t * P:(t + 1) * P],
                                  y[:, bass.ds(of[t], D)], start=True, stop=True)
                    last.then_inc(group_used, 1)
            pe.wait_ge(idx_staged, (STAGE_NO[TO_SRC] + 1) * GROUPS)
            pe.wait_ge(map_loaded, 48)
            convolve(BY_SRC)
            dense(5, x)
            with pe.Fori(0, ROUNDS) as i:
                for s in range(SLOTS):
                    at = i * ROUND + s * G
                    pe.wait_ge(hot_ready, EDGE * GROUPS + i * SLOTS + s + 1)
                    pe.wait_ge(gathered[s], (GATHER_NO[EDGE] * ROUNDS + i + 1) * (G * 16))
                    for t in range(G + 2):
                        if t < G:
                            pe.wait_ge(q_copied, at + t + 1)
                            if t >= 2:
                                pe.wait_ge(edge_hidden, at + t - 1)
                            z = bank(t % 2)[0:D, 0:P]
                            mm(z, ring[:, s, t, 0:D], ident[:, :], start=True, stop=False)
                            mm(z, q_now[:, t % 4, :], hotT[:, s, t * P:(t + 1) * P], start=False, stop=True)\
                                .then_inc(edge_sums, 1)
                        if 1 <= t <= G:
                            u = t - 1
                            pe.wait_ge(edge_hidden, at + u + 1)
                            if u >= 2:
                                pe.wait_ge(msg_ready, at + u - 1)
                            mm(bank(2 + u % 2)[:, 0:D], hT[:, u % 2, :], e2[:, :],
                               start=True, stop=True).then_inc(msg_sums, 1)
                        if t >= 2:
                            u = t - 2
                            pe.wait_ge(msg_ready, at + u + 1)
                            pe.wait_ge(tile_added, at + u + 1)
                            last = mm(bank(4 + u % 2)[:, 0:ROW], hot[:, s, u, :], msg[:, u % 4, :],
                                      start=True, stop=True)
                            if u < G - 1:
                                last.then_inc(tile_sums, 1)
                    last.then_inc(tile_sums, 1)
                    pe.sem_inc(group_used, 1)


_ORDER = ["x_in", "src_in", "dst_in", "w_in", "mats_in", "rows_in", "qb_in", "e2b_in"]


def kernel(**inputs):
    import concourse.bacc as bacc
    from concourse.bass_utils import run_bass_kernel_spmd

    a = {k: np.asarray(v) for k, v in inputs.items()}

    def edges(v, pad):
        whole = np.full(P * ROWS_IN, pad, v.dtype)
        whole[:N_EDGES] = v
        return whole.reshape(ROWS_IN, P)

    xs = np.zeros((P * BLOCKS, D), a["x"].dtype)
    xs[:N_NODES] = a["x"]
    ww = [a["L1_gnn_Ww0"], a["L1_gnn_Ww1"]]
    by_name = {
        "c1_rel": a["L0_gnn_W1_rel"], "c1_root": a["L0_gnn_W1_root"],
        "c2_rel": a["L0_gnn_W2_rel"], "c2_root": a["L0_gnn_W2_root"],
        "q0": a["L1_gnn_Qw0"].T, "wa0": ww[0][:, :D].T, "wb0": ww[0][:, D:].T,
        "q1": a["L1_gnn_Qw1"].T, "wa1": ww[1][:, :D].T, "wb1": ww[1][:, D:].T,
        "bi1": a["L2_gnn_W1"].T, "bi2": a["L2_gnn_W2"].T,
        "e1a": a["L3_gnn_W1"][:D], "e1b": a["L3_gnn_W1"][D:], "e2": a["L3_gnn_W2"],
    }
    biases = {"c1": "L0_gnn_b1", "c2": "L0_gnn_b2", "w0": "L1_gnn_Wb0", "w1": "L1_gnn_Wb1",
              "bi1": "L2_gnn_b1", "bi2": "L2_gnn_b2", "e1": "L3_gnn_b1"}
    arrays = {
        "x_in": xs.reshape(BLOCKS, P, D).transpose(1, 0, 2).reshape(P, BLOCKS * D),
        "src_in": edges(a["src"], PAD_NODE), "dst_in": edges(a["dst"], PAD_NODE),
        "w_in": edges(a["edge_weight"], 0),
        "mats_in": np.stack([by_name[n] for n in MATS], axis=1),
        "rows_in": np.stack([a[biases[n]] for n in ROWS]),
        "qb_in": np.stack([a["L1_gnn_Qb0"], a["L1_gnn_Qb1"]], axis=1),
        "e2b_in": a["L3_gnn_b2"][None],
    }
    arrays = {k: np.ascontiguousarray(v) for k, v in arrays.items()}
    nc = bacc.Bacc("TRN2", target_bir_lowering=False, num_devices=1)
    args = [nc.dram_tensor(k, arrays[k].shape, mybir.dt.from_np(arrays[k].dtype), kind="ExternalInput").ap()
            for k in _ORDER]
    out = nc.dram_tensor("out", [P, BLOCKS * D], F32, kind="ExternalOutput").ap()
    build(nc, *args, out)
    got = run_bass_kernel_spmd(nc, [arrays], core_ids=[0]).results[0]["out"]
    return got.reshape(P, BLOCKS, D).transpose(1, 0, 2).reshape(P * BLOCKS, D)[:N_NODES]
```

```python
import numpy as np
import concourse.bass as bass
from concourse import mybir
from concourse.alu_op_type import AluOpType as ALU

F32, I32, BF16 = mybir.dt.float32, mybir.dt.int32, mybir.dt.bfloat16
ACT = mybir.ActivationFunctionType
AX = mybir.AxisListType
PE_ENGINE, ACT_ENGINE, DVE_ENGINE = (
    mybir.EngineType.PE, mybir.EngineType.Activation, mybir.EngineType.DVE)

P = 128
N_NODES, N_EDGES, D = 6250, 206250, 64
BLOCKS = -(-N_NODES // P)
COLS = -(-N_EDGES // P)
G, SLOTS = 8, 4
ROUND = G * SLOTS
TILES = -(-(COLS + BLOCKS) // ROUND) * ROUND
ROUNDS = TILES // ROUND
GROUPS = TILES // G
G0 = 13
ROUNDS0 = COLS // (G0 * SLOTS)
BK = ROUNDS
TCH = TILES // P
BANK = 512
PER_BANK, ACC = 7, 72
NBANK = BLOCKS // PER_BANK
LAST_PLACE = (NBANK - 1) * BANK + (PER_BANK - 1) * ACC
ROW = D + 1
PAD_NODE, PAD_LOW = 8191, 200.0
CH = 4
CHUNKS = 2 * NBANK
LAYERS = 6
EPS, SLOPE = 1e-5, 0.01
PARTS = ((0, 3), (3, NBANK - 1), (NBANK - 1, NBANK))
NORM_AT = (24, 47)
DENSE_AT = (48, 49)
EARLY = 2 * (NBANK - 1)
assert COLS == G0 * SLOTS * ROUNDS0 and NBANK * PER_BANK == BLOCKS and TCH * P == TILES
assert BK >= BLOCKS and P * BLOCKS <= PAD_NODE < P * 64

MATS = ["c1_rel", "c1_root", "c2_rel", "c2_root", "q0", "wa0", "wb0", "q1", "wa1", "wb1",
        "bi1", "bi2", "e1a", "e1b", "e2"]
ROWS = ["c1", "c2", "w0", "w1", "bi1", "bi2", "e1"]


class Steps:

    def __init__(self, engine, sem):
        self.engine, self.sem, self.n = engine, sem, 0

    def __call__(self, instruction):
        instruction.then_inc(self.sem, 1)
        self.n = self.n + 1
        self.engine.wait_ge(self.sem, self.n)

    def loop(self, begin, end, each, body):
        first = self.n
        with self.engine.Fori(begin, end) as i:
            self.n = first + (i - begin) * each
            body(i)
        self.n = first + (end - begin) * each


def chunk_blocks(c):
    return PER_BANK * (c // 2) + CH * (c % 2), CH if c % 2 == 0 else PER_BANK - CH


def stretches():
    at, out = 0, []
    for r in NORM_AT + DENSE_AT:
        if at < r:
            out.append((at, r, None))
        out.append((r, r + 1, r))
        at = r + 1
    return out + [(at, ROUNDS, None)]


ROWS_IN = TILES + 2


def build(nc, x_in, src_in, dst_in, w_in, mats_in, rows_in, qb_in, e2b_in, out):
    from contextlib import ExitStack
    ctx = ExitStack()
    with ctx:
        def sb(name, shape, dt=F32):
            return ctx.enter_context(nc.sbuf_tensor(name, shape, dt))

        def sem(name):
            return ctx.enter_context(nc.semaphore(name))

        tables = [nc.dram_tensor(f"table{k}", [P * BLOCKS, D], F32, kind="Internal").ap() for k in range(2)]
        slots_d = nc.dram_tensor("slots_d", [P * TILES, 3], F32, kind="Internal").ap()
        rows_d = nc.dram_tensor("rows_d", [P * TILES, ROW], F32, kind="Internal").ap()
        low_d = nc.dram_tensor("low_d", [TILES, P], F32, kind="Internal").ap()
        place_d = nc.dram_tensor("place_d", [3, TCH, P], I32, kind="Internal").ap()

        row_iota = sb("row_iota", [P, P])
        part_iota = sb("part_iota", [P, 1])
        block_iota = sb("block_iota", [P, BK])
        tile_iota = sb("tile_iota", [P, TCH])
        ident = sb("ident", [P, P])
        before = sb("before", [P, P])
        ones = sb("ones", [P, P])
        zeros = sb("zeros", [P, BANK])
        mats = sb("mats", [D, len(MATS), D])
        rows = sb("rows", [P, len(ROWS), D])
        qb = sb("qb", [D, 2])
        bi_stack = sb("bi_stack", [P, D])
        edge_w = sb("edge_w", [D, 2, D])
        e2 = sb("e2", [ROW, D])

        def rectangle(rows):
            return rows.rearrange("r e -> (r e)")[0:P * COLS].rearrange("(p j) -> p j", p=P)

        wide = sb("wide", [P, 2 * SLOTS * G * P])
        src_i = wide[:, 0:COLS].bitcast(I32)
        dst_i = wide[:, COLS:2 * COLS].bitcast(I32)
        w_raw = wide[:, 2 * COLS:3 * COLS]
        hotT = wide[:, 0:SLOTS * G * P].rearrange("p (s e) -> p s e", s=SLOTS)
        lowT = wide[:, SLOTS * G * P:].rearrange("p (s e) -> p s e", s=SLOTS)
        half = wide[:, :].bitcast(BF16)
        src_hot = half[:, 0:SLOTS * G * P].rearrange("p (s g e) -> p s g e", s=SLOTS, g=G)
        src_blk = half[:, SLOTS * G * P:SLOTS * G * (P + BLOCKS)]\
            .rearrange("p (s g b) -> p s g b", s=SLOTS, g=G)
        low_turn = wide[:, 0:4 * P].rearrange("p (a e) -> p a e", e=P)
        pairs = wide[:, 0:BLOCKS * 2 * D].rearrange("p (b f) -> p b f", b=BLOCKS)

        sorting = sb("sorting", [P, 4, TILES])
        blk, member, run, rank = (sorting[:, k, :] for k in range(4))
        edge_acc = sorting[:, :, :].rearrange("p a k -> p (a k)")[:, 0:NBANK * BANK]
        count = sb("count", [P, BK])
        total = sb("total", [P, BK])
        totals = sb("totals", [P, BK])[:, :]
        total_i = sb("total_i", [P, BK], I32)
        base = sb("base", [P, BK])
        first_tile = sb("first_tile", [P, BK])
        edge0 = sb("edge0", [P, TCH])
        edge0_i = sb("edge0_i", [P, TCH], I32)
        offset = sb("offset", [P, TCH])
        row_of = sb("row_of", [P, TCH, 2], I32)
        next_dst = sb("next_dst", [P, 1], I32)
        next_blk = sb("next_blk", [P, 1])
        shift = sb("shift", [P, 2, BK])
        disorder = sb("disorder", [P, 1], I32)
        uneven = sb("uneven", [P, 2], I32)
        bound = sb("bound", [P, 2])
        window_out = sb("window_out", [P, SLOTS, 3, P])
        started = member[:, 0:TCH * (BLOCKS - 1)].rearrange("p (c b) -> p c b", c=TCH)
        map_f = sb("map_f", [P, TCH])
        map_i = sb("map_i", [P, 3, TCH], I32)
        pos = sb("pos", [P, TILES], I32)

        slots = sb("slots", [P, TILES, 3])
        gidx = sb("gidx", [P, TILES], I32)
        low = sb("low", [P, TILES])
        weight = sb("weight", [P, TILES])
        src_low = sb("src_low", [P, TILES])
        place = sb("place", [1, 3, TILES], I32)

        x = sb("x", [P, BLOCKS * D])
        r = sb("r", [P, BLOCKS * D])
        spent = slots[:, :, :].rearrange("p k w -> p (k w)")
        y = spent[:, 0:BLOCKS * D]
        dinv = sb("dinv", [P, BLOCKS])
        stat = sb("stat", [P, 4, BLOCKS])
        xT = spent[:, BLOCKS * D:BLOCKS * D + 3 * BANK].rearrange("p (a n) -> p a n", a=3)
        qT = sb("qT", [D, 2, BANK])

        ring = sb("ring", [P, SLOTS, G, ROW])
        hot = sb("hot", [P, SLOTS, G, P])
        h_wide = wide[:, SLOTS * G * P:SLOTS * G * P + BLOCKS * D]
        h_sorting = edge_acc[:, 0:BLOCKS * D]
        h_beside = sorting[:, :, :].rearrange("p a k -> p (a k)")[:, NBANK * BANK:]
        h_hot = hot[:, :, :, :].rearrange("p s g e -> p (s g e)")[:, 0:BLOCKS * D]
        idx_ring = sb("idx_ring", [P, SLOTS, G0], I32)
        rec_ring = sb("rec_ring", [P, SLOTS, G0, 3])
        q_now = sb("q_now", [P, 4, D])
        hT = sb("hT", [ROW, 2, P])
        msg = sb("msg", [P, 4, ROW])

        acc = ctx.enter_context(nc.psum_tensor("acc", [P, 8 * BANK], F32))
        spare = acc[:, NBANK * BANK:]

        def bank(k):
            return acc[:, k * BANK:(k + 1) * BANK]

        def by_node(t):
            return t.rearrange("p (k n) -> p k n", n=BANK)[:, :, 0:PER_BANK * ACC]\
                .rearrange("p k (j f) -> p k j f", f=ACC)

        sums = by_node(acc[:, 0:NBANK * BANK])

        def nodes(t):
            return t.rearrange("p (k j f) -> p k j f", k=NBANK, j=PER_BANK)

        def mat(name):
            return mats[:, MATS.index(name), :]

        def bias(name, n):
            i = ROWS.index(name)
            return rows[:, i:i + 1, :].to_broadcast([P, n, D])

        in_dst, in_edges, in_nodes, in_weights = sem("in_dst"), sem("in_edges"), sem("in_nodes"), sem("in_weights")
        fetched = [sem(f"fetched{s}") for s in range(SLOTS)]
        rows_known, window_made, window_turned, window_laid = (
            sem("rows_known"), sem("window_made"), sem("window_turned"), sem("window_laid"))
        window_low_stored = [sem(f"window_low_stored{s}") for s in range(SLOTS)]
        order_known, recs_cleared = sem("order_known"), sem("recs_cleared")
        evenness_known, dve_node_step = sem("evenness_known"), sem("dve_node_step")
        sent = [sem(f"sent{s}") for s in range(SLOTS)]
        rank_turn = sem("rank_turn")
        dve_sort_step = sem("dve_sort_step")
        iotas, consts, padded, pad_stored = sem("iotas"), sem("consts"), sem("padded"), sem("pad_stored")
        counted, base_sums, map_made, map_stored = (
            sem("counted"), sem("base_sums"), sem("map_made"), sem("map_stored"))
        map_loaded, recs_made, recs_staged = sem("map_loaded"), sem("recs_made"), sem("recs_staged")
        scattered = [sem(f"scattered{s}") for s in range(SLOTS)]
        slots_loaded, derived = sem("slots_loaded"), sem("derived")
        low_turned, low_copied, low_stored = sem("low_turned"), sem("low_copied"), [
            sem(f"low_stored{s}") for s in range(SLOTS)]
        rows_cleared = sem("rows_cleared")
        nodes_ready, turned, turned_out = sem("nodes_ready"), sem("turned"), sem("turned_out")
        q_sums, q_biased, q_ready = sem("q_sums"), sem("q_biased"), sem("q_ready")
        dense_sums, dense_out = sem("dense_sums"), sem("dense_out")
        table_stored = sem("table_stored")
        idx_staged, hot_ready, group_used = sem("idx_staged"), sem("hot_ready"), sem("group_used")
        gathered = [sem(f"gathered{s}") for s in range(SLOTS)]
        low_loaded = [sem(f"low_loaded{s}") for s in range(SLOTS)]
        rows_loaded = [sem(f"rows_loaded{s}") for s in range(SLOTS)]
        deg_summed = sem("deg_summed")
        pos2_made = sem("pos2_made")
        q_copied, edge_sums, edge_hidden = sem("q_copied"), sem("edge_sums"), sem("edge_hidden")
        msg_sums, msg_ready, tile_sums = sem("msg_sums"), sem("msg_ready"), sem("tile_sums")
        tile_added = sem("tile_added")
        root_in, root_out, done, stored = sem("root_in"), sem("root_out"), sem("done"), sem("stored")
        dve_step, act_step, pool_step = sem("dve_step"), sem("act_step"), sem("pool_step")

        CONV1, CONV2, MEAN1, MEAN2, TO_SRC, BY_SRC, EDGE = range(7)
        GATHER_NO = {CONV1: 0, CONV2: 1, MEAN1: 2, MEAN2: 3, EDGE: 4}
        STAGE_NO = {CONV1: 0, CONV2: 1, MEAN1: 2, MEAN2: 3, TO_SRC: 4, EDGE: 5}
        ROOT_NO = {CONV2: 0, MEAN1: 4, MEAN2: 7, BY_SRC: 13, EDGE: 20}
        DEGREE_ROOT = 3
        TABLE_OF = {0: 0, 1: 1, 2: 0, 3: 1, 5: 0}

        def unordered(engine):
            engine.wait_ge(order_known, 1)
            return engine.If(engine.value_load(disorder[0:1, 0:1], min_val=0, max_val=1) > 0)

        def even_blocks(engine, yes=True):
            engine.wait_ge(evenness_known, 1)
            k = 1 if yes else 0
            return engine.If(engine.value_load(uneven[0:1, k:k + 1], min_val=0, max_val=1) > 0)

        block = ctx.enter_context(nc.Block())

        @block.sync
        def _(sp):
            for to, of in ((dst_i, dst_in), (src_i, src_in), (w_raw, w_in)):
                sp.dma_start(to, rectangle(of)).then_inc(in_dst if of is dst_in else in_edges, 16)
                if of is dst_in:
                    sp.dma_start(x[:, :], x_in).then_inc(in_nodes, 16)
            sp.wait_ge(consts, 1)
            with nc.allow_non_contiguous_dma(reason="one number for each partition"):
                sp.dma_start(next_dst[0:P - 1, :],
                             dst_in.rearrange("r e -> (r e)")[COLS:P * COLS]
                             .rearrange("(p j) -> p j", j=COLS)[:, 0:1]).then_inc(in_dst, 16)
            sp.dma_start(mats[:, :, :], mats_in).then_inc(in_weights, 16)
            sp.dma_start(rows[:, :, :], rows_in.partition_broadcast(P)).then_inc(in_weights, 16)
            sp.dma_start(qb[:, :], qb_in).then_inc(in_weights, 16)
            sp.dma_start(bi_stack[0:D, :], mats_in[:, MATS.index("bi1"), :]).then_inc(in_weights, 16)
            sp.dma_start(bi_stack[D:2 * D, :], mats_in[:, MATS.index("bi2"), :]).then_inc(in_weights, 16)
            sp.dma_start(e2[0:D, :], mats_in[:, MATS.index("e2"), :]).then_inc(in_weights, 16)
            sp.dma_start(e2[D:ROW, :], e2b_in).then_inc(in_weights, 16)
            def store_table(layer):
                to = tables[TABLE_OF[layer]].rearrange("(p b) f -> p (b f)", p=P)
                cut = PARTS[-1][0] * PER_BANK * D
                sp.wait_ge(dense_out, CHUNKS * layer + EARLY)
                sp.dma_start(to[:, 0:cut], y[:, 0:cut]).then_inc(table_stored, 16)
                sp.wait_ge(dense_out, CHUNKS * (layer + 1))
                sp.dma_start(to[:, cut:], y[:, cut:]).then_inc(table_stored, 16)

            def turn_map(n, which):
                sp.wait_ge(map_made, n + 1)
                with nc.allow_non_contiguous_dma(reason="a small table"):
                    for i, m in enumerate(which):
                        sp.dma_start(place_d[m].rearrange("c p -> p c"), map_i[:, m, :])\
                            .then_inc(map_stored, 16)
                    sp.wait_ge(map_stored, 32 if n == 0 else 48)
                for i, m in enumerate(which):
                    sp.dma_start(place[0:1, m, :], place_d[m].rearrange("c p -> (c p)").unsqueeze(0))\
                        .then_inc(map_loaded, 16)

            store_table(0)
            turn_map(0, (0, 1))
            for c in range(TCH):
                sp.wait_ge(window_made, c + 1)
                sp.dma_start(low_d[c * P:(c + 1) * P, :], window_out[:, c % SLOTS, 1, :])\
                    .then_inc(window_low_stored[c % SLOTS], 16)
            for s in range(SLOTS):
                sp.wait_ge(window_low_stored[s], 16 * -(-(TCH - s) // SLOTS))
            with unordered(sp):
                sp.wait_ge(recs_cleared, 1)
                sp.dma_start(slots_d.rearrange("(p k) w -> p (k w)", p=P),
                             slots[:, :, :].rearrange("p k w -> p (k w)")).then_inc(pad_stored, 16)
                for s in range(SLOTS):
                    sp.wait_ge(scattered[s], ROUNDS0 * G0 * 16)
                sp.dma_start(slots[:, :, :].rearrange("p k w -> p (k w)"),
                             slots_d.rearrange("(p k) w -> p (k w)", p=P)).then_inc(slots_loaded, 16)
                for c in range(TCH):
                    sp.wait_ge(low_copied, c + 1)
                    sp.dma_start(low_d[c * P:(c + 1) * P, :], low_turn[:, c % SLOTS, :])\
                        .then_inc(low_stored[c % SLOTS], 16)
                for s in range(SLOTS):
                    sp.wait_ge(low_stored[s], 16 * -(-(TCH - s) // SLOTS))

            wide_rows = rows_d.rearrange("(p k) w -> p (k w)", p=P)
            sp.wait_ge(padded, 1)
            with sp.Fori(0, ROUNDS) as i:
                sp.wait_ge(group_used, CONV1 * GROUPS + i * SLOTS + 1)
                sp.dma_start(wide_rows[:, bass.ds(i * (ROUND * ROW), ROUND * ROW)]
                             .rearrange("p (a w) -> p a w", w=4 * ROW),
                             msg[:, :, :].rearrange("p a w -> p (a w)").unsqueeze(1)
                             .to_broadcast([P, ROUND // 4, 4 * ROW])).then_inc(rows_cleared, 16)
            store_table(1)
            turn_map(1, (2,))
            store_table(2)
            store_table(3)

            def load_low(edge_pass, n):
                with sp.Fori(0, ROUNDS) as i:
                    for s in range(SLOTS):
                        sp.wait_ge(group_used, edge_pass * GROUPS + i * SLOTS + s + 1)
                        sp.dma_start(lowT[:, s, :],
                                     low_d[bass.ds(i * ROUND + s * G, G), :].rearrange("k e -> (k e)")
                                     .partition_broadcast(P)).then_inc(low_loaded[s], 16)

            sp.wait_ge(turned, CHUNKS * 5)
            load_low(TO_SRC, 0)
            for s in range(SLOTS):
                sp.wait_ge(sent[s], ROUNDS * G * 16)
            with sp.Fori(0, ROUNDS) as i:
                for s in range(SLOTS):
                    sp.wait_ge(group_used, BY_SRC * GROUPS + i * SLOTS + s + 1)
                    sp.dma_start(ring[:, s, :, :].rearrange("p g w -> p (g w)"),
                                 wide_rows[:, bass.ds((i * ROUND + s * G) * ROW, G * ROW)])\
                        .then_inc(rows_loaded[s], 16)
            store_table(5)
            load_low(EDGE, 1)
            cut = PARTS[-1][0] * PER_BANK * D
            sp.wait_ge(done, 1)
            sp.dma_start(out[:, 0:cut], x[:, 0:cut]).then_inc(stored, 16)
            sp.wait_ge(done, 2)
            sp.dma_start(out[:, cut:], x[:, cut:]).then_inc(stored, 16)
            sp.wait_ge(stored, 32)
            sp.wait_ge(rows_cleared, 16 * ROUNDS)

        @block.gpsimd
        def _(pool):
            pool.iota(row_iota[:, :], [[1, P]], base=0, channel_multiplier=0,
                      allow_small_or_imprecise_dtypes=True).then_inc(iotas, 1)
            pool.iota(part_iota[:, :], [[1, 1]], base=0, channel_multiplier=1,
                      allow_small_or_imprecise_dtypes=True).then_inc(iotas, 1)
            pool.iota(block_iota[:, :], [[1, BK]], base=0, channel_multiplier=0,
                      allow_small_or_imprecise_dtypes=True).then_inc(iotas, 1)
            pool.iota(tile_iota[:, :], [[P, TCH]], base=0, channel_multiplier=1,
                      allow_small_or_imprecise_dtypes=True).then_inc(iotas, 1)
            pool.wait_ge(rows_known, 1)
            for c in range(TCH):
                if c >= SLOTS:
                    pool.wait_ge(window_made, c - SLOTS + 1)
                for k, of in enumerate((src_in, dst_in, w_in)):
                    for j in range(2):
                        to = hot[:, c % SLOTS, 2 * k + j, :]
                        pool.indirect_dma_start(
                            to if of is w_in else to.bitcast(I32), None, of,
                            bass.IndirectOffsetOnAxis(row_of[:, c, j:j + 1], 0)
                        ).then_inc(fetched[c % SLOTS], 16)
            with unordered(pool):
                pool.wait_ge(pad_stored, 16)
                with pool.Fori(0, ROUNDS0) as i:
                    for s in range(SLOTS):
                        pool.wait_ge(recs_staged, i * SLOTS + s + 1)
                        pool.sem_inc(pool_step, 1)
                        for t in range(G0):
                            pool.indirect_dma_start(
                                slots_d, bass.IndirectOffsetOnAxis(idx_ring[:, s, t:t + 1], 0),
                                rec_ring[:, s, t, :], None, bounds_check=P * TILES - 1, oob_is_err=False
                            ).then_inc(scattered[s], 16)

            def gather(edge_pass, stored_tables):
                table = tables[(stored_tables - 1) % 2]
                pool.wait_ge(table_stored, 32 * stored_tables)
                first = STAGE_NO[edge_pass] * GROUPS
                with pool.Fori(0, ROUNDS) as i:
                    for s in range(SLOTS):
                        pool.wait_ge(idx_staged, first + i * SLOTS + s + 1)
                        pool.sem_inc(pool_step, 1)
                        for t in range(G):
                            pool.indirect_dma_start(
                                ring[:, s, t, 0:D], None, table,
                                bass.IndirectOffsetOnAxis(idx_ring[:, s, t:t + 1], 0)
                            ).then_inc(gathered[s], 16)

            gather(CONV1, 1)
            gather(CONV2, 2)
            gather(MEAN1, 3)
            gather(MEAN2, 4)
            pool.wait_ge(rows_cleared, 16 * ROUNDS)
            first = STAGE_NO[TO_SRC] * GROUPS
            with pool.Fori(0, ROUNDS) as i:
                for s in range(SLOTS):
                    pool.wait_ge(idx_staged, first + i * SLOTS + s + 1)
                    pool.sem_inc(pool_step, 1)
                    for t in range(G):
                        pool.indirect_dma_start(
                            rows_d, bass.IndirectOffsetOnAxis(idx_ring[:, s, t:t + 1], 0),
                            ring[:, s, t, :], None, bounds_check=P * TILES - 1, oob_is_err=False
                        ).then_inc(sent[s], 16)
            gather(EDGE, 5)

        @block.scalar
        def _(act):
            step = Steps(act, act_step)

            def roots(n, part=(0, NBANK)):
                cols = slice(part[0] * PER_BANK, part[1] * PER_BANK)
                act.wait_ge(root_in, n + 1)
                nc.scalar.activation(stat[:, 3, cols], stat[:, 2, cols], ACT.Sqrt).then_inc(root_out, 1)

            def part_roots(edge_pass, j):
                if edge_pass == MEAN2:
                    roots(ROOT_NO[MEAN2] + 2 * j, PARTS[j])
                    roots(ROOT_NO[MEAN2] + 2 * j + 1, PARTS[j])
                elif edge_pass != CONV1:
                    roots(ROOT_NO[edge_pass] + j, PARTS[j])

            def dense(layer, c0=0, c1=CHUNKS):
                mid = layer in (2, 3)
                width = 2 * D if layer == 4 else D
                for c in range(c0, c1 + 1):
                    n = layer * CHUNKS + c
                    if c < c1:
                        cols = chunk_blocks(c)[1] * P
                        act.wait_ge(turned, n + 1)
                        if n >= 3:
                            act.wait_ge(dense_sums, n - 2)
                        nc.scalar.copy(xT[0:width, n % 3, 0:cols], bank(n % 2)[0:width, 0:cols])\
                            .then_inc(turned_out, 1)
                    if mid and c > c0:
                        cols = chunk_blocks(c - 1)[1] * P
                        q = (layer - 2) * CHUNKS + c - 1
                        act.wait_ge(q_sums, q + 1)
                        if c >= 3:
                            act.wait_ge(dense_sums, n - 2)
                        nc.scalar.activation(qT[:, q % 2, 0:cols], bank(2 + q % 2)[0:D, 0:cols],
                                             ACT.Identity, bias=qb[:, layer - 2:layer - 1])\
                            .then_inc(q_biased, 1)

            dense(0, 0, EARLY)
            dense(0, EARLY, CHUNKS)
            act.wait_ge(table_stored, 32)
            for c in range(TCH):
                act.wait_ge(window_turned, c + 1)
                nc.scalar.copy(slots[:, c * P:(c + 1) * P, :],
                               bank(c % 4)[:, 0:3 * P].rearrange("p (w k) -> p k w", w=3))\
                    .then_inc(window_laid, 1)

            with unordered(act):
                act.wait_ge(recs_made, 1)

                def stage_records(i, waits):
                    for s in range(SLOTS):
                        at = i * SLOTS * G0 + s * G0
                        if waits:
                            act.wait_ge(scattered[s], i * (G0 * 16))
                        nc.scalar.copy(idx_ring[:, s, :], pos[:, bass.ds(at, G0)])
                        nc.scalar.copy(rec_ring[:, s, :, :], slots[:, bass.ds(at, G0), :])\
                            .then_inc(recs_staged, 1)

                stage_records(0, False)
                with act.Fori(1, ROUNDS0) as i:
                    stage_records(i, True)
                for c in range(TCH):
                    act.wait_ge(low_turned, c + 1)
                    if c >= SLOTS:
                        act.wait_ge(low_stored[c % SLOTS], 16 * (c // SLOTS))
                    nc.scalar.copy(low_turn[:, c % SLOTS, :], bank(c % 4)[:, 0:P]).then_inc(low_copied, 1)

            def node_work(edge_pass, layer, r):
                with even_blocks(act):
                    if r in NORM_AT:
                        part_roots(edge_pass, NORM_AT.index(r))
                    else:
                        half = EARLY // len(DENSE_AT)
                        j = DENSE_AT.index(r)
                        dense(layer, j * half, (j + 1) * half)

            def late_work(edge_pass, layer):
                with even_blocks(act, yes=False):
                    part_roots(edge_pass, 0)
                    part_roots(edge_pass, 1)
                    dense(layer, 0, EARLY)
                part_roots(edge_pass, 2)
                dense(layer, EARLY, CHUNKS)

            def stage_indices(edge_pass, layer):
                def stage_round(i):
                    for s in range(SLOTS):
                        act.wait_ge(group_used, edge_pass * GROUPS + i * SLOTS + s + 1)
                        nc.scalar.copy(idx_ring[:, s, 0:G], gidx[:, bass.ds(i * ROUND + s * G, G)])\
                            .then_inc(idx_staged, 1)

                for begin, end, work in stretches():
                    if work is None:
                        with act.Fori(begin, end) as i:
                            stage_round(i)
                    else:
                        stage_round(begin)
                        node_work(edge_pass, layer, work)
                late_work(edge_pass, layer)

            act.wait_ge(derived, 1)
            stage_indices(CONV1, 1)
            stage_indices(CONV2, 2)
            roots(DEGREE_ROOT)
            stage_indices(MEAN1, 3)
            stage_indices(MEAN2, 4)
            act.wait_ge(pos2_made, 1)

            def send_rows(i, waits):
                for s in range(SLOTS):
                    at = i * ROUND + s * G
                    act.wait_ge(group_used, SLOTS + TO_SRC * GROUPS + i * SLOTS + s + 1)
                    if waits:
                        act.wait_ge(sent[s], i * (G * 16))
                    nc.scalar.copy(ring[:, s, :, 0:D], bank(s).rearrange("p (g f) -> p g f", g=G))
                    nc.scalar.copy(ring[:, s, :, D:ROW], src_low[:, bass.ds(at, G)].unsqueeze(2))
                    nc.scalar.copy(idx_ring[:, s, 0:G], pos[:, bass.ds(at, G)]).then_inc(idx_staged, 1)

            send_rows(0, False)
            with act.Fori(1, ROUNDS) as i:
                send_rows(i, True)
            for k in range(NBANK):
                roots(ROOT_NO[BY_SRC] + k, (k, k + 1))
                dense(5, 2 * k, 2 * k + 2)
            AHEAD = SLOTS - 1

            def edge_indices(n, at):
                act.wait_ge(group_used, EDGE * GROUPS + n + 1)
                nc.scalar.copy(idx_ring[:, at % SLOTS, 0:G], gidx[:, bass.ds(n * G, G)])\
                    .then_inc(idx_staged, 1)

            def edge_round(i, last):
                at, of = i * ROUND, {}

                def copy_q(t):
                    s = t // G
                    if s not in of:
                        of[s] = nc.values_load_multi_w_load_instructions(
                            place[0:1, 1, bass.ds(at + s * G, G)], engines=(ACT_ENGINE,), min_val=0,
                            max_val=(BLOCKS - 1) * D, skip_runtime_bounds_check_because="counted blocks")[1]
                    if t >= 4:
                        act.wait_ge(edge_sums, at + t - 3)
                    nc.scalar.copy(q_now[:, t % 4, :], r[:, bass.ds(of[s][t % G], D)]).then_inc(q_copied, 1)

                for t in range(3):
                    copy_q(t)
                for t in range(ROUND):
                    if t + 3 < ROUND:
                        copy_q(t + 3)
                    act.wait_ge(edge_sums, at + t + 1)
                    if t >= 2:
                        act.wait_ge(msg_sums, at + t - 1)
                    nc.scalar.activation(hT[0:D, t % 2, :], bank(t % 2)[0:D, 0:P],
                                         ACT.Relu).then_inc(edge_hidden, 1)
                    s = t // G
                    if t % G == 2 and (not last or s + AHEAD < SLOTS):
                        edge_indices(i * SLOTS + s + AHEAD, s + AHEAD)

            for n in range(AHEAD):
                edge_indices(n, n)
            act.wait_ge(dense_out, CHUNKS * LAYERS)
            at = 0
            for j, until in enumerate(NORM_AT):
                with act.Fori(at, until) as i:
                    edge_round(i, False)
                with even_blocks(act):
                    part_roots(EDGE, j)
                at = until
            with act.Fori(at, ROUNDS - 1) as i:
                edge_round(i, False)
            edge_round(ROUNDS - 1, True)
            with even_blocks(act, yes=False):
                part_roots(EDGE, 0)
                part_roots(EDGE, 1)
            part_roots(EDGE, 2)

        @block.vector
        def _(dve):
            step = Steps(dve, dve_step)
            v = nc.vector

            dve.sem_inc(tile_added, 2)
            v.memset(next_dst[:, :], PAD_NODE)
            v.memset(zeros[:, :], 0.0).then_inc(consts, 1)
            dve.wait_ge(iotas, 4)
            v.memset(ones[:, :], 1.0).then_inc(consts, 1)
            v.tensor_scalar(ident[:, :], row_iota[:, :], part_iota[:, :], None, ALU.is_equal)\
                .then_inc(consts, 1)
            v.tensor_scalar(before[:, :], row_iota[:, :], part_iota[:, :], None, ALU.is_gt)\
                .then_inc(consts, 1)
            v.memset(hT[D:ROW, :, :], 1.0).then_inc(consts, 1)
            v.memset(ring[:, :, :, D:ROW], 1.0).then_inc(consts, 1)
            dve.sem_inc(nodes_ready, 2)
            step(v.memset(msg[:, :, 0:D], 0.0))
            v.memset(msg[:, :, D:ROW], PAD_LOW).then_inc(padded, 1)

            node = Steps(dve, dve_node_step)

            def dense(layer, c0=0, c1=CHUNKS):
                mid = layer in (2, 3)
                for c in range(c0, c1 + 1):
                    if mid and c < c1:
                        cols = chunk_blocks(c)[1] * P
                        q = (layer - 2) * CHUNKS + c
                        dve.wait_ge(q_biased, q + 1)
                        v.scalar_tensor_tensor(qT[:, q % 2, 0:cols], qT[:, q % 2, 0:cols], SLOPE,
                                               qT[:, q % 2, 0:cols], ALU.mult, ALU.max).then_inc(q_ready, 1)
                    if c > c0:
                        b0, n = chunk_blocks(c - 1)
                        dve.wait_ge(dense_sums, layer * CHUNKS + c)
                        both = bank(4 + (layer * CHUNKS + c - 1) % 2)[:, 0:n * P]\
                            .rearrange("p (b w) -> p b w", b=n)
                        yv = y[:, b0 * D:(b0 + n) * D].rearrange("p (b f) -> p b f", b=n)
                        rv = r[:, b0 * D:(b0 + n) * D].rearrange("p (b f) -> p b f", b=n)
                        if layer == 4:
                            v.tensor_tensor(yv, both[:, :, 0:D],
                                            dinv[:, b0:b0 + n].unsqueeze(2).to_broadcast([P, n, D]), ALU.mult)
                            node(v.tensor_tensor(rv, both[:, :, D:], bias("bi1", n), ALU.add))
                            v.tensor_tensor(rv, rv, bias("bi2", n), ALU.add).then_inc(dense_out, 1)
                        else:
                            v.tensor_copy(yv, both[:, :, 0:D])
                            name = {0: "c1", 1: "c2", 2: "w0", 3: "w1", 5: "e1"}[layer]
                            v.tensor_tensor(rv, both[:, :, D:], bias(name, n), ALU.add)\
                                .then_inc(dense_out, 1)

            def count_block(b, cols):
                step(v.tensor_scalar(member[:, 0:cols], blk[:, 0:cols], block_iota[:, bass.ds(b, 1)],
                                     None, ALU.is_equal, ALU.add, accum_out=count[:, bass.ds(b, 1)]))

            COUNT_STEPS = 1

            def rank_block(step, b, cols):
                step(v.tensor_scalar(member[:, 0:cols], blk[:, 0:cols], block_iota[:, bass.ds(b, 1)],
                                     None, ALU.is_equal))
                step(v.tensor_tensor_scan(run[:, 0:cols], member[:, 0:cols], member[:, 0:cols],
                                          base[:, bass.ds(b, 1)], ALU.add, ALU.max))
                dve.sem_inc(rank_turn, 1)
                step(v.copy_predicated(rank[:, 0:cols], member[:, 0:cols].bitcast(I32), run[:, 0:cols]))

            RANK_STEPS = 3

            def bases(n):
                v.engine_nop().then_inc(counted, 1)
                dve.wait_ge(base_sums, n + 1)
                step(v.tensor_copy(totals, spare[:, 64:64 + BK]))
                step(v.tensor_scalar(total[:, :], totals, float(P - 1), None, ALU.add))
                step(v.tensor_copy(total_i[:, :], total[:, :]))
                step(v.tensor_scalar(total_i[:, :], total_i[:, :], 7, None, ALU.arith_shift_right))
                step(v.tensor_copy(total[:, :], total_i[:, :]))
                step(v.tensor_tensor_scan(first_tile[:, :], total[:, :], total[:, :], 0.0, ALU.add, ALU.max))
                step(v.tensor_tensor(first_tile[:, :], first_tile[:, :], total[:, :], ALU.subtract))
                step(v.scalar_tensor_tensor(base[:, :], first_tile[:, :], float(P), spare[:, 0:BK],
                                            ALU.mult, ALU.add))
                step(v.tensor_tensor(
                    started, tile_iota[:, :].unsqueeze(2).to_broadcast([P, TCH, BLOCKS - 1]),
                    first_tile[:, None, 1:BLOCKS].to_broadcast([P, TCH, BLOCKS - 1]), ALU.is_ge))
                step(v.tensor_reduce(map_f[:, :], started, AX.X, ALU.add))
                m = 1 if n == 0 else 2
                step(v.tensor_scalar(map_i[:, m, :], map_f[:, :], float(D), None, ALU.mult))
                to = 0 if n == 0 else 2
                step(v.tensor_scalar(total_i[:, 0:TCH], map_f[:, :], 37.0, None, ALU.mult))
                step(v.tensor_scalar(total_i[:, 0:TCH], total_i[:, 0:TCH], 8, None, ALU.arith_shift_right))
                step(v.tensor_copy(total[:, 0:TCH], total_i[:, 0:TCH]))
                step(v.tensor_scalar(total[:, 0:TCH], total[:, 0:TCH], float(BANK - PER_BANK * ACC), None,
                                     ALU.mult))
                v.scalar_tensor_tensor(map_i[:, to, :], map_f[:, :], float(ACC), total[:, 0:TCH],
                                       ALU.mult, ALU.add).then_inc(map_made, 1)

            def evenness():
                for j in range(2):
                    end = PARTS[j][1] * PER_BANK
                    step(v.tensor_scalar(bound[:, j:j + 1], first_tile[:, end:end + 1],
                                         float(NORM_AT[j] * ROUND), None, ALU.is_gt))
                step(v.tensor_tensor(bound[:, 0:1], bound[:, 0:1], bound[:, 1:2], ALU.max))
                step(v.tensor_scalar(bound[:, 1:2], bound[:, 0:1], 0.0, None, ALU.is_equal))
                v.tensor_copy(uneven[:, :], bound[:, :]).then_inc(evenness_known, 1)

            def slot_numbers(step, cols):
                step(v.tensor_scalar(rank[:, 0:cols], rank[:, 0:cols], -1.0, None, ALU.add))
                step(v.tensor_copy(member[:, 0:cols].bitcast(I32), rank[:, 0:cols]))
                step(v.tensor_scalar(pos[:, 0:cols], member[:, 0:cols].bitcast(I32), P - 1, None,
                                     ALU.bitwise_and))
                step(v.tensor_copy(rank[:, 0:cols], pos[:, 0:cols]))
                step(v.tensor_scalar(pos[:, 0:cols], member[:, 0:cols].bitcast(I32), 7, None,
                                     ALU.arith_shift_right))
                step(v.tensor_copy(run[:, 0:cols], pos[:, 0:cols]))
                step(v.scalar_tensor_tensor(run[:, 0:cols], rank[:, 0:cols], float(TILES), run[:, 0:cols],
                                            ALU.mult, ALU.add))
                step(v.tensor_scalar(rank[:, 0:cols], blk[:, 0:cols], float(BLOCKS), 1e6, ALU.is_ge,
                                     ALU.mult))
                return v.tensor_tensor(pos[:, 0:cols], run[:, 0:cols], rank[:, 0:cols], ALU.add)

            dve.wait_ge(in_dst, 32)
            step(v.memset(count[:, :], 0.0))
            step(v.tensor_scalar(pos[:, 0:COLS], dst_i, 7, None, ALU.arith_shift_right))
            step(v.tensor_copy(blk[:, 0:COLS], pos[:, 0:COLS]))
            step(v.tensor_scalar(next_dst[:, :], next_dst[:, :], 7, None, ALU.arith_shift_right))
            step(v.tensor_copy(next_blk[:, :], next_dst[:, :]))
            step(v.tensor_tensor(member[:, 0:COLS - 1], blk[:, 1:COLS], blk[:, 0:COLS - 1], ALU.is_lt))
            step(v.tensor_tensor(member[:, COLS - 1:COLS], next_blk[:, :], blk[:, COLS - 1:COLS], ALU.is_lt))
            step(v.tensor_reduce(count[:, BLOCKS:BLOCKS + 1], member[:, 0:COLS], AX.X, ALU.add))
            blk_half = run[:, 0:COLS].bitcast(BF16)[:, 0:COLS]
            member_half = member[:, 0:COLS].bitcast(BF16)[:, 0:COLS]
            step(v.tensor_copy(blk_half, blk[:, 0:COLS]))
            dve.wait_ge(in_weights, 16 * 7)
            for k in range(NBANK):
                for j in range(PER_BANK):
                    b = k * PER_BANK + j
                    step(v.tensor_scalar(member_half, blk_half, block_iota[:, b:b + 1], None,
                                         ALU.is_equal, ALU.add, accum_out=count[:, b:b + 1]))
                dense(0, 2 * k, 2 * k + 2)
            bases(0)
            starts, grows = shift[:, 0, :], shift[:, 1, :]
            step(v.tensor_tensor_scan(starts, totals, totals, 0.0, ALU.add, ALU.max))
            step(v.tensor_tensor(starts, starts, totals, ALU.subtract))
            step(v.scalar_tensor_tensor(starts, first_tile[:, :], -float(P), starts, ALU.mult, ALU.add))
            step(v.tensor_tensor(grows[:, 1:BLOCKS], starts[:, 1:BLOCKS], starts[:, 0:BLOCKS - 1],
                                 ALU.subtract))
            step(v.tensor_tensor(started, started,
                                 shift[:, 1:2, 1:BLOCKS].to_broadcast([P, TCH, BLOCKS - 1]), ALU.mult))
            step(v.tensor_reduce(edge0[:, :], started, AX.X, ALU.add))
            step(v.scalar_tensor_tensor(edge0[:, :], tile_iota[:, :], float(P), edge0[:, :],
                                        ALU.mult, ALU.add))
            step(v.tensor_copy(edge0_i[:, :], edge0[:, :]))
            step(v.tensor_scalar(row_of[:, :, 0], edge0_i[:, :], 7, None, ALU.arith_shift_right))
            step(v.tensor_copy(edge0[:, :], row_of[:, :, 0]))
            step(v.tensor_scalar(edge0_i[:, :], edge0_i[:, :], P - 1, None, ALU.bitwise_and))
            step(v.tensor_copy(offset[:, :], edge0_i[:, :]))
            v.tensor_scalar(row_of[:, :, 1], edge0[:, :], 1.0, None, ALU.add).then_inc(rows_known, 1)
            for c in range(TCH):
                s = c % SLOTS
                part = [hot[:, s, j, :] for j in range(G)]
                src2, dst2, w2, mask, wrong = part[1], part[3], part[5], part[6], part[7]
                o_src, o_low, o_w = (window_out[:, s, k, :] for k in range(3))
                dve.wait_ge(fetched[s], 96 * (c // SLOTS + 1))
                step(v.tensor_scalar(mask, row_iota[:, :], offset[:, c:c + 1], None, ALU.is_ge))
                if c >= SLOTS:
                    dve.wait_ge(window_turned, c - SLOTS + 1)
                    dve.wait_ge(window_low_stored[s], 16 * (c // SLOTS))
                v.copy_predicated(src2, mask.bitcast(I32), part[0])
                v.copy_predicated(w2, mask.bitcast(I32), part[4])
                step(v.copy_predicated(dst2, mask.bitcast(I32), part[2]))
                v.tensor_copy(o_src, src2.bitcast(I32))
                v.tensor_copy(o_w, w2)
                v.tensor_scalar(part[2].bitcast(I32), dst2.bitcast(I32), 7, None, ALU.arith_shift_right)
                step(v.tensor_scalar(part[0].bitcast(I32), dst2.bitcast(I32), P - 1, None, ALU.bitwise_and))
                step(v.tensor_scalar(wrong, part[2].bitcast(I32), map_f[:, c:c + 1], None, ALU.not_equal))
                v.scalar_tensor_tensor(o_src, wrong, float(PAD_NODE), o_src, ALU.mult, ALU.max)
                v.scalar_tensor_tensor(o_low, wrong, PAD_LOW, part[0].bitcast(I32), ALU.mult, ALU.max)\
                    .then_inc(window_made, 1)
            step(v.tensor_scalar(shift[:, 0, 0:1], totals[:, BLOCKS:BLOCKS + 1], 1.0, None, ALU.min))
            v.tensor_copy(disorder[:, :], shift[:, 0, 0:1]).then_inc(order_known, 1)
            evenness()
            dve.wait_ge(window_laid, TCH)
            with unordered(dve):
                sort_step = Steps(dve, dve_sort_step)
                dve.wait_ge(in_edges, 32)
                v.memset(slots[:, :, 0:1], float(PAD_NODE))
                v.memset(slots[:, :, 1:2], PAD_LOW)
                v.memset(slots[:, :, 2:3], 0.0).then_inc(recs_cleared, 1)
                sort_step(v.memset(rank[:, :], 0.0))
                sort_step.loop(0, BLOCKS, RANK_STEPS, lambda b: rank_block(sort_step, b, COLS))
                sort_step(slot_numbers(sort_step, COLS))
                dve.wait_ge(pad_stored, 16)
                sort_step(v.tensor_scalar(member[:, 0:COLS].bitcast(I32), dst_i, P - 1, None,
                                          ALU.bitwise_and))
                v.tensor_copy(slots[:, 0:COLS, 0:1], src_i.unsqueeze(2))
                v.tensor_copy(slots[:, 0:COLS, 1:2], member[:, 0:COLS].bitcast(I32).unsqueeze(2))
                v.tensor_copy(slots[:, 0:COLS, 2:3], w_raw.unsqueeze(2)).then_inc(recs_made, 1)
                dve.wait_ge(slots_loaded, 16)
                dve.wait_ge(low_copied, TCH)
                for s in range(SLOTS):
                    dve.wait_ge(low_stored[s], 16 * -(-(TCH - s) // SLOTS))

            v.tensor_copy(low[:, :], slots[:, :, 1])
            v.tensor_copy(weight[:, :], slots[:, :, 2])
            step(v.tensor_copy(pos[:, :], slots[:, :, 0]))
            step(v.tensor_scalar(gidx[:, :], pos[:, :], P - 1, None, ALU.bitwise_and))
            step(v.tensor_copy(src_low[:, :], gidx[:, :]))
            step(v.tensor_scalar(gidx[:, :], pos[:, :], 7, None, ALU.arith_shift_right))
            step(v.tensor_copy(blk[:, :], gidx[:, :]))
            step(v.scalar_tensor_tensor(member[:, :], src_low[:, :], float(BLOCKS), blk[:, :],
                                        ALU.mult, ALU.add))
            v.tensor_scalar(gidx[:, :], member[:, :], float(P * BLOCKS - 1), None, ALU.min)\
                .then_inc(derived, 1)
            step(v.memset(count[:, :], 0.0))
            step(v.memset(rank[:, :], 0.0))

            def hots(s, at, numbers, weighted):
                ins = v.tensor_tensor(
                    hot[:, s, :, :], row_iota[:, None, :].to_broadcast([P, G, P]),
                    numbers.unsqueeze(2).to_broadcast([P, G, P]), ALU.is_equal)
                if weighted:
                    step(ins)
                    ins = v.tensor_tensor(
                        hot[:, s, :, :], hot[:, s, :, :],
                        weight[:, bass.ds(at, G)].unsqueeze(2).to_broadcast([P, G, P]), ALU.mult)
                return ins

            def flat(part, t):
                return t[:, part[0] * PER_BANK * D:part[1] * PER_BANK * D]

            def of_part(part, t):
                return flat(part, t).rearrange("p (k j f) -> p k j f", j=PER_BANK, f=D)

            def column(part, t, k):
                return t[:, k, part[0] * PER_BANK:part[1] * PER_BANK]\
                    .rearrange("p (k j) -> p k j", j=PER_BANK)

            def wide_stat(part, k):
                return column(part, stat, k).unsqueeze(3)\
                    .to_broadcast([P, part[1] - part[0], PER_BANK, D])

            def part_sums(part, of=None):
                return (sums if of is None else of)[:, part[0]:part[1]]

            def root(n):
                v.engine_nop().then_inc(root_in, 1)
                dve.wait_ge(root_out, n + 1)

            def relu_sums(part, h):
                node(v.tensor_tensor(of_part(part, h), part_sums(part)[:, :, :, 0:D],
                                     of_part(part, r[:, :]), ALU.add))
                node(v.tensor_scalar(flat(part, h), flat(part, h), 0.0, None, ALU.max))

            def layer_norm(n, part, h):
                xf, hf = flat(part, x[:, :]), flat(part, h)
                s0, s1, s2, s3 = (column(part, stat, k) for k in range(4))
                node(v.tensor_tensor(xf, xf, hf, ALU.add))
                node(v.tensor_reduce(s0, of_part(part, x[:, :]), AX.X, ALU.add))
                node(v.tensor_scalar(s0, s0, 1.0 / D, None, ALU.mult))
                node(v.tensor_tensor(of_part(part, x[:, :]), of_part(part, x[:, :]), wide_stat(part, 0),
                                     ALU.subtract))
                node(v.tensor_tensor(hf, xf, xf, ALU.mult))
                node(v.tensor_reduce(s1, of_part(part, h), AX.X, ALU.add))
                node(v.tensor_scalar(s2, s1, 1.0 / D, EPS, ALU.mult, ALU.add))
                root(n)
                node(v.reciprocal(s0, s3))
                node(v.tensor_tensor(of_part(part, x[:, :]), of_part(part, x[:, :]), wide_stat(part, 0),
                                     ALU.mult))

            def mean_norm(n, part, h):
                wsum = part_sums(part)[:, :, :, D]
                s0, s1, s2, s3 = (column(part, stat, k) for k in range(4))
                hf, rf = flat(part, h), flat(part, r[:, :])
                node(v.tensor_scalar(s0, wsum, 0.0, None, ALU.is_equal))
                node(v.tensor_tensor(s0, s0, wsum, ALU.add))
                node(v.reciprocal(s1, s0))
                node(v.tensor_tensor(of_part(part, h), part_sums(part)[:, :, :, 0:D], wide_stat(part, 1),
                                     ALU.mult))
                node(v.tensor_tensor(hf, hf, rf, ALU.add))
                node(v.scalar_tensor_tensor(hf, hf, SLOPE, hf, ALU.mult, ALU.max))
                node(v.tensor_tensor(rf, hf, hf, ALU.mult))
                node(v.tensor_reduce(s2, of_part(part, r[:, :]), AX.X, ALU.add))
                root(n)
                node(v.tensor_scalar(s0, s3, 0.0, None, ALU.is_equal))
                node(v.tensor_tensor(s0, s0, s3, ALU.add))
                node(v.reciprocal(s1, s0))
                node(v.tensor_tensor(of_part(part, h), of_part(part, h), wide_stat(part, 1), ALU.mult))

            def norms(edge_pass, j):
                part = PARTS[j]
                if edge_pass == CONV1:
                    relu_sums(part, h_wide)
                elif edge_pass == CONV2:
                    relu_sums(part, h_wide)
                    layer_norm(ROOT_NO[CONV2] + j, part, h_wide)
                elif edge_pass == MEAN1:
                    mean_norm(ROOT_NO[MEAN1] + j, part, h_wide)
                elif edge_pass == MEAN2:
                    mean_norm(ROOT_NO[MEAN2] + 2 * j, part, h_wide)
                    layer_norm(ROOT_NO[MEAN2] + 2 * j + 1, part, h_wide)
                    xb = flat(part, x[:, :]).rearrange("p (b f) -> p b f", f=D)
                    beside = pairs[:, part[0] * PER_BANK:part[1] * PER_BANK, :]
                    v.tensor_copy(beside[:, :, 0:D], xb)
                    node(v.tensor_tensor(beside[:, :, D:], xb, xb, ALU.mult))
                elif edge_pass == EDGE:
                    sums_here = part_sums(part, by_node(edge_acc))
                    h = h_hot if j == 2 else h_beside
                    node(v.tensor_scalar(column(part, stat, 0), sums_here[:, :, :, D], 1.0, None, ALU.max))
                    node(v.reciprocal(column(part, stat, 1), column(part, stat, 0)))
                    node(v.tensor_tensor(of_part(part, h), sums_here[:, :, :, 0:D], wide_stat(part, 1),
                                         ALU.mult))
                    layer_norm(ROOT_NO[EDGE] + j, part, h)

            def ready():
                v.engine_nop().then_inc(nodes_ready, 1)

            def node_work(edge_pass, layer, at):
                with even_blocks(dve):
                    if at in NORM_AT:
                        norms(edge_pass, NORM_AT.index(at))
                        if at == NORM_AT[-1]:
                            ready()
                    else:
                        half = EARLY // len(DENSE_AT)
                        j = DENSE_AT.index(at)
                        dense(layer, j * half, (j + 1) * half)

            def pass_rounds(edge_pass, layer, each, body, extra=None):
                first = node.n
                for begin, end, work in stretches():
                    if work is None:
                        step.loop(begin, end, each, body)
                    else:
                        body(begin)
                        node_work(edge_pass, layer, work)
                        if extra is not None and work == NORM_AT[0]:
                            extra()
                dve.wait_ge(group_used, SLOTS + (edge_pass + 1) * GROUPS)
                node.n = first
                with even_blocks(dve, yes=False):
                    norms(edge_pass, 0)
                    norms(edge_pass, 1)
                    ready()
                    dense(layer, 0, EARLY)
                norms(edge_pass, 2)
                ready()
                dense(layer, EARLY, CHUNKS)

            def convolve(edge_pass, layer, weighted=False, more=None, more_steps=0, extra=None):
                def body(i):
                    for s in range(SLOTS):
                        at = i * ROUND + s * G
                        dve.wait_ge(group_used, edge_pass * GROUPS + i * SLOTS + s + 1)
                        if edge_pass == CONV2:
                            v.tensor_tensor(
                                src_hot[:, s, :, :], row_iota[:, None, :].to_broadcast([P, G, P]),
                                src_low[:, bass.ds(at, G)].unsqueeze(2).to_broadcast([P, G, P]),
                                ALU.is_equal)
                            v.tensor_tensor(
                                src_blk[:, s, :, :],
                                block_iota[:, None, 0:BLOCKS].to_broadcast([P, G, BLOCKS]),
                                blk[:, bass.ds(at, G)].unsqueeze(2).to_broadcast([P, G, BLOCKS]),
                                ALU.is_equal)
                        hots(s, at, low[:, bass.ds(at, G)], weighted).then_inc(hot_ready, 1)
                    if more is not None:
                        more(i)

                pass_rounds(edge_pass, layer, more_steps + (SLOTS if weighted else 0), body, extra)

            dve.wait_ge(in_weights, 16 * 7)
            v.tensor_tensor(edge_w[:, 0, :], mat("e1a"), mat("e1b"), ALU.subtract)
            step(v.tensor_copy(edge_w[:, 1, :], mat("e1b")))
            convolve(CONV1, 1, more=lambda i: count_block(i, TILES), more_steps=COUNT_STEPS)
            bases(1)
            convolve(CONV2, 2, more=lambda i: rank_block(step, i, TILES), more_steps=RANK_STEPS)
            dve.wait_ge(deg_summed, 1)
            step(v.tensor_copy(dinv[:, :], spare[:, 128:128 + BLOCKS]))
            step(v.tensor_scalar(stat[:, 2, :], dinv[:, :], 1.0, None, ALU.max))
            root(DEGREE_ROOT)
            step(v.reciprocal(stat[:, 0, :], stat[:, 3, :]))
            step(v.tensor_scalar(stat[:, 1, :], dinv[:, :], 0.0, None, ALU.is_gt))
            step(v.tensor_tensor(dinv[:, :], stat[:, 0, :], stat[:, 1, :], ALU.mult))

            def number_slots():
                step(slot_numbers(step, TILES))
                v.engine_nop().then_inc(pos2_made, 1)

            convolve(MEAN1, 3, weighted=True, extra=number_slots)
            convolve(MEAN2, 4, weighted=True)

            def turned_hots(n, i, s):
                dve.wait_ge(low_loaded[s], (n * ROUNDS + i + 1) * 16)
                return v.tensor_scalar(hotT[:, s, :], lowT[:, s, :], part_iota[:, :], None, ALU.is_equal)

            with dve.Fori(0, ROUNDS) as i:
                for s in range(SLOTS):
                    turned_hots(0, i, s).then_inc(hot_ready, 1)

            def by_source(i):
                for s in range(SLOTS):
                    dve.wait_ge(rows_loaded[s], (i + 1) * 16)
                    dve.wait_ge(group_used, BY_SRC * GROUPS + i * SLOTS + s + 1)
                    hots(s, None, ring[:, s, :, D], False).then_inc(hot_ready, 1)

            with dve.Fori(0, ROUNDS) as i:
                by_source(i)
            dve.wait_ge(group_used, SLOTS + (BY_SRC + 1) * GROUPS)
            every = (0, NBANK)
            db = dinv[:, :].rearrange("p (k j) -> p k j", j=PER_BANK).unsqueeze(3)\
                .to_broadcast([P, NBANK, PER_BANK, D])
            node(v.tensor_tensor(of_part(every, h_sorting), part_sums(every)[:, :, :, 0:D], db, ALU.mult))
            node(v.tensor_tensor(h_sorting, h_sorting, r[:, :], ALU.add))
            for k in range(NBANK):
                layer_norm(ROOT_NO[BY_SRC] + k, (k, k + 1), h_sorting)
                ready()
                if k >= 1:
                    dense(5, 2 * k - 2, 2 * k)
            dense(5, CHUNKS - 2, CHUNKS)
            first = EDGE * GROUPS
            step(v.memset(edge_acc, 0.0))
            dve.wait_ge(rows_cleared, 16 * ROUNDS)
            step(v.memset(msg[:, :, :], 1.0))

            HOTS_AT = (0, 1, 3, 5)
            PART = G // len(HOTS_AT)

            def edge_hots(i, s, k):
                if k == 0:
                    dve.wait_ge(group_used, first + i * SLOTS + s + 1)
                    dve.wait_ge(low_loaded[s], (ROUNDS + i + 1) * 16)
                along = slice(k * PART * P, (k + 1) * PART * P)
                v.tensor_scalar(hotT[:, s, along], lowT[:, s, along], part_iota[:, :], None, ALU.is_equal)
                ins = v.tensor_tensor(
                    hot[:, s, k * PART:(k + 1) * PART, :],
                    row_iota[:, None, :].to_broadcast([P, PART, P]),
                    low[:, bass.ds(i * ROUND + s * G + k * PART, PART)].unsqueeze(2)
                    .to_broadcast([P, PART, P]), ALU.is_equal)
                if k == len(HOTS_AT) - 1:
                    ins.then_inc(hot_ready, 1)

            def edge_round(i, last):
                at, to = i * ROUND, {}
                for t in range(ROUND + 1):
                    s, u = divmod(t, G)
                    if t < ROUND:
                        if u == 0:
                            to[s] = nc.values_load_multi_w_load_instructions(
                                place[0:1, 0, bass.ds(at + s * G, G)], engines=(DVE_ENGINE,), min_val=0,
                                max_val=LAST_PLACE, skip_runtime_bounds_check_because="counted blocks")[1]
                        dve.wait_ge(msg_sums, at + t + 1)
                        v.tensor_scalar(msg[:, t % 4, 0:D], bank(2 + t % 2)[:, 0:D], 0.0,
                                        None, ALU.max).then_inc(msg_ready, 1)
                    if t >= 1:
                        dve.wait_ge(tile_sums, at + t)
                        here = edge_acc[:, bass.ds(to[(t - 1) // G][(t - 1) % G], ROW)]
                        v.tensor_tensor(here, here, bank(4 + (t - 1) % 2)[:, 0:ROW], ALU.add)\
                            .then_inc(tile_added, 1)
                        dve.wait_ge(tile_added, at + t + 2)
                    if t < ROUND and u in HOTS_AT:
                        if s + 1 < SLOTS:
                            edge_hots(i, s + 1, HOTS_AT.index(u))
                        elif not last:
                            edge_hots(i + 1, 0, HOTS_AT.index(u))

            for k in range(len(HOTS_AT)):
                edge_hots(0, 0, k)
            at, before_norms = 0, node.n
            for j, until in enumerate(NORM_AT):
                with dve.Fori(at, until) as i:
                    edge_round(i, False)
                with even_blocks(dve):
                    norms(EDGE, j)
                at = until
            with dve.Fori(at, ROUNDS - 1) as i:
                edge_round(i, False)
            edge_round(ROUNDS - 1, True)
            node.n = before_norms
            with even_blocks(dve, yes=False):
                norms(EDGE, 0)
                norms(EDGE, 1)
            v.engine_nop().then_inc(done, 1)
            norms(EDGE, 2)
            v.engine_nop().then_inc(done, 1)

        @block.tensor
        def _(pe):
            mm = nc.tensor.matmul
            pe.sem_inc(group_used, SLOTS)
            pe.wait_ge(consts, 6)

            def base_products(n):
                pe.wait_ge(counted, n + 1)
                mm(spare[:, 0:BK], before[:, :], count[:, :], start=True, stop=True)
                mm(spare[:, 64:64 + BK], ones[:, :], count[:, :], start=True, stop=True)\
                    .then_inc(base_sums, 1)

            pe.wait_ge(in_weights, 16 * 7)
            pe.wait_ge(in_nodes, 16)

            def dense(layer, source, c0, c1):
                mid = layer in (2, 3)
                width = 2 * D if layer == 4 else D
                lag = 2 if mid else 1
                if layer < 5:
                    pe.wait_ge(nodes_ready, 2 * layer + (1 if c1 <= EARLY else 2))
                else:
                    pe.wait_ge(nodes_ready, 2 * layer + c1 // 2)
                for c in range(c0, c1 + lag):
                    n = layer * CHUNKS + c
                    if c < c1:
                        if n >= 2:
                            pe.wait_ge(turned_out, n - 1)
                        for t in range(chunk_blocks(c)[1]):
                            b = chunk_blocks(c)[0] + t
                            last = mm(bank(n % 2)[0:width, t * P:(t + 1) * P],
                                      source[:, b * width:(b + 1) * width], ident[:, :],
                                      start=True, stop=True)
                        last.then_inc(turned, 1)
                    if mid and c0 < c <= c1:
                        q = (layer - 2) * CHUNKS + c - 1
                        cols = chunk_blocks(c - 1)[1] * P
                        pe.wait_ge(turned_out, n)
                        if q >= 2:
                            pe.wait_ge(q_biased, q - 1)
                        mm(bank(2 + q % 2)[0:D, 0:cols], mat("q0" if layer == 2 else "q1"),
                           xT[0:D, (n - 1) % 3, 0:cols], start=True, stop=True).then_inc(q_sums, 1)
                    if c >= c0 + lag:
                        m = n - lag
                        pe.wait_ge(turned_out, m + 1)
                        if mid:
                            q = (layer - 2) * CHUNKS + c - lag
                            pe.wait_ge(q_ready, q + 1)
                        if m >= 2:
                            pe.wait_ge(dense_out, m - 1)
                        for t in range(chunk_blocks(c - lag)[1]):
                            tile = slice(t * P, (t + 1) * P)
                            own = xT[0:D, m % 3, tile]
                            left, right = bank(4 + m % 2)[:, t * P:t * P + D], \
                                bank(4 + m % 2)[:, t * P + D:(t + 1) * P]
                            if layer in (0, 1, 5):
                                k = 0 if layer == 5 else MATS.index(("c1_rel", "c2_rel")[layer])
                                both = (edge_w if layer == 5 else mats)[:, k:k + 2, :]
                                last = mm(bank(4 + m % 2)[:, tile], own, both.rearrange("p a f -> p (a f)"),
                                          start=True, stop=True)
                                continue
                            if mid:
                                k = layer - 2
                                pairs_of = (qT[:, q % 2, tile], mat(f"wb{k}")), (own, mat(f"wa{k}"))
                            else:
                                pairs_of = (xT[:, m % 3, tile], bi_stack[:, :]), (own, mat("bi1"))
                            mm(left, *pairs_of[0], start=True, stop=True)
                            last = mm(right, *pairs_of[1], start=True, stop=True)
                        last.then_inc(dense_sums, 1)
                pe.wait_ge(dense_out, layer * CHUNKS + c1)

            dense(0, x, 0, EARLY)
            dense(0, x, EARLY, CHUNKS)
            base_products(0)
            for c in range(TCH):
                pe.wait_ge(window_made, c + 1)
                if c >= 4:
                    pe.wait_ge(window_laid, c - 3)
                for k in range(3):
                    last = mm(bank(c % 4)[:, k * P:(k + 1) * P], window_out[:, c % SLOTS, k, :], ident[:, :],
                              start=True, stop=True)
                last.then_inc(window_turned, 1)
            pe.wait_ge(window_laid, TCH)
            with unordered(pe):
                pe.wait_ge(slots_loaded, 16)
                for c in range(TCH):
                    if c >= 4:
                        pe.wait_ge(low_copied, c - 3)
                    mm(bank(c % 4)[:, 0:P], slots[:, c * P:(c + 1) * P, 1], ident[:, :],
                       start=True, stop=True).then_inc(low_turned, 1)
                pe.wait_ge(low_copied, TCH)
            pe.wait_ge(map_loaded, 32)

            def clear_sums(times=1):
                for _ in range(times):
                    for k in range(NBANK):
                        mm(bank(k), zeros[:, 0:P], zeros[:, :], start=True, stop=True)

            def blocks_of(which, at):
                _, values = nc.values_load_multi_w_load_instructions(
                    place[0:1, which, bass.ds(at, G)], engines=(PE_ENGINE,), min_val=0,
                    max_val=(BLOCKS - 1) * D if which == 1 else LAST_PLACE,
                    skip_runtime_bounds_check_because="counted blocks")
                return values

            SOURCE = {1: h_wide, 2: x, 3: h_wide, 4: wide, 5: x}

            def convolve(edge_pass, layer):
                if edge_pass == BY_SRC:
                    pe.wait_ge(hot_ready, BY_SRC * GROUPS + 1)
                clear_sums(3 if edge_pass == BY_SRC else 1)
                if edge_pass == CONV2:
                    mm(spare[:, 128:128 + BLOCKS], zeros[:, 0:P], zeros[:, 0:BLOCKS], start=True, stop=True)
                columns = ROW if edge_pass in (MEAN1, MEAN2) else D

                def groups(i, slots):
                    for s in slots:
                        at = i * ROUND + s * G
                        to = blocks_of(2 if edge_pass == BY_SRC else 0, at)
                        pe.wait_ge(hot_ready, edge_pass * GROUPS + i * SLOTS + s + 1)
                        if edge_pass != BY_SRC:
                            pe.wait_ge(gathered[s], (GATHER_NO[edge_pass] * ROUNDS + i + 1) * (G * 16))
                        for t in range(G):
                            if edge_pass == CONV2:
                                mm(spare[:, 128:128 + BLOCKS], src_hot[:, s, t, :], src_blk[:, s, t, :],
                                   start=False, stop=True, skip_group_check=True)
                            last = mm(acc[:, bass.ds(to[t], columns)], hot[:, s, t, :],
                                      ring[:, s, t, 0:columns],
                                      start=False, stop=True, skip_group_check=True)
                        last.then_inc(group_used, 1)

                if edge_pass == BY_SRC:
                    with pe.Fori(0, ROUNDS) as i:
                        groups(i, range(SLOTS))
                    for k in range(NBANK):
                        dense(layer, SOURCE[layer], 2 * k, 2 * k + 2)
                    return
                half = EARLY // len(DENSE_AT)
                for begin, end, work in stretches():
                    if work is None or work in NORM_AT:
                        with pe.Fori(begin, end) as i:
                            groups(i, range(SLOTS))
                    else:
                        groups(begin, range(1))
                        j = DENSE_AT.index(work)
                        with even_blocks(pe):
                            dense(layer, SOURCE[layer], j * half, (j + 1) * half)
                        groups(begin, range(1, SLOTS))
                if edge_pass == CONV2:
                    mm(spare[:, 64:65], zeros[:, 0:P], zeros[:, 0:1], start=True, stop=True)\
                        .then_inc(deg_summed, 1)
                with even_blocks(pe, yes=False):
                    dense(layer, SOURCE[layer], 0, EARLY)
                dense(layer, SOURCE[layer], EARLY, CHUNKS)

            convolve(CONV1, 1)
            base_products(1)
            pe.wait_ge(map_made, 2)
            convolve(CONV2, 2)
            convolve(MEAN1, 3)
            convolve(MEAN2, 4)
            with pe.Fori(0, ROUNDS) as i:
                for s in range(SLOTS):
                    of = blocks_of(1, i * ROUND + s * G)
                    pe.wait_ge(hot_ready, TO_SRC * GROUPS + i * SLOTS + s + 1)
                    pe.wait_ge(idx_staged, STAGE_NO[TO_SRC] * GROUPS + i * SLOTS + s + 1 - SLOTS)
                    for t in range(G):
                        last = mm(bank(s)[:, t * D:(t + 1) * D], hotT[:, s, t * P:(t + 1) * P],
                                  y[:, bass.ds(of[t], D)], start=True, stop=True)
                    last.then_inc(group_used, 1)
            pe.wait_ge(idx_staged, (STAGE_NO[TO_SRC] + 1) * GROUPS)
            pe.wait_ge(map_loaded, 48)
            convolve(BY_SRC, 5)
            with pe.Fori(0, ROUNDS) as i:
                at = i * ROUND
                for t in range(ROUND + 2):
                    s, g = divmod(t, G)
                    if t < ROUND:
                        if g == 0:
                            pe.wait_ge(hot_ready, EDGE * GROUPS + i * SLOTS + s + 1)
                            pe.wait_ge(gathered[s], (GATHER_NO[EDGE] * ROUNDS + i + 1) * (G * 16))
                        pe.wait_ge(q_copied, at + t + 1)
                        if t >= 2:
                            pe.wait_ge(edge_hidden, at + t - 1)
                        z = bank(t % 2)[0:D, 0:P]
                        mm(z, ring[:, s, g, 0:D], ident[:, :], start=True, stop=False)
                        mm(z, q_now[:, t % 4, :], hotT[:, s, g * P:(g + 1) * P], start=False, stop=True)\
                            .then_inc(edge_sums, 1)
                    if 1 <= t <= ROUND:
                        u = t - 1
                        pe.wait_ge(edge_hidden, at + u + 1)
                        if u >= 2:
                            pe.wait_ge(msg_ready, at + u - 1)
                        mm(bank(2 + u % 2)[:, 0:D], hT[:, u % 2, :], e2[:, :],
                           start=True, stop=True).then_inc(msg_sums, 1)
                    if t >= 2:
                        u = t - 2
                        pe.wait_ge(msg_ready, at + u + 1)
                        pe.wait_ge(tile_added, at + u + 1)
                        mm(bank(4 + u % 2)[:, 0:ROW], hot[:, u // G, u % G, :], msg[:, u % 4, :],
                           start=True, stop=True).then_inc(tile_sums, 1)
                        if u % G == G - 1:
                            pe.sem_inc(group_used, 1)


_ORDER = ["x_in", "src_in", "dst_in", "w_in", "mats_in", "rows_in", "qb_in", "e2b_in"]


def kernel(**inputs):
    import concourse.bacc as bacc
    from concourse.bass_utils import run_bass_kernel_spmd

    a = {k: np.asarray(v) for k, v in inputs.items()}

    def edges(v, pad):
        whole = np.full(P * ROWS_IN, pad, v.dtype)
        whole[:N_EDGES] = v
        return whole.reshape(ROWS_IN, P)

    xs = np.zeros((P * BLOCKS, D), a["x"].dtype)
    xs[:N_NODES] = a["x"]
    ww = [a["L1_gnn_Ww0"], a["L1_gnn_Ww1"]]
    by_name = {
        "c1_rel": a["L0_gnn_W1_rel"], "c1_root": a["L0_gnn_W1_root"],
        "c2_rel": a["L0_gnn_W2_rel"], "c2_root": a["L0_gnn_W2_root"],
        "q0": a["L1_gnn_Qw0"].T, "wa0": ww[0][:, :D].T, "wb0": ww[0][:, D:].T,
        "q1": a["L1_gnn_Qw1"].T, "wa1": ww[1][:, :D].T, "wb1": ww[1][:, D:].T,
        "bi1": a["L2_gnn_W1"].T, "bi2": a["L2_gnn_W2"].T,
        "e1a": a["L3_gnn_W1"][:D], "e1b": a["L3_gnn_W1"][D:], "e2": a["L3_gnn_W2"],
    }
    biases = {"c1": "L0_gnn_b1", "c2": "L0_gnn_b2", "w0": "L1_gnn_Wb0", "w1": "L1_gnn_Wb1",
              "bi1": "L2_gnn_b1", "bi2": "L2_gnn_b2", "e1": "L3_gnn_b1"}
    arrays = {
        "x_in": xs.reshape(BLOCKS, P, D).transpose(1, 0, 2).reshape(P, BLOCKS * D),
        "src_in": edges(a["src"], PAD_NODE), "dst_in": edges(a["dst"], PAD_NODE),
        "w_in": edges(a["edge_weight"], 0),
        "mats_in": np.stack([by_name[n] for n in MATS], axis=1),
        "rows_in": np.stack([a[biases[n]] for n in ROWS]),
        "qb_in": np.stack([a["L1_gnn_Qb0"], a["L1_gnn_Qb1"]], axis=1),
        "e2b_in": a["L3_gnn_b2"][None],
    }
    arrays = {k: np.ascontiguousarray(v) for k, v in arrays.items()}
    nc = bacc.Bacc("TRN2", target_bir_lowering=False, num_devices=1)
    args = [nc.dram_tensor(k, arrays[k].shape, mybir.dt.from_np(arrays[k].dtype), kind="ExternalInput").ap()
            for k in _ORDER]
    out = nc.dram_tensor("out", [P, BLOCKS * D], F32, kind="ExternalOutput").ap()
    build(nc, *args, out)
    got = run_bass_kernel_spmd(nc, [arrays], core_ids=[0]).results[0]["out"]
    return got.reshape(P, BLOCKS, D).transpose(1, 0, 2).reshape(P * BLOCKS, D)[:N_NODES]
```
